# Optimizing a Trainium2 kernel written in Bass

```python
import numpy as np
import jax
import jax.numpy as jnp

def _softmax(x, axis=-1):
    return jax.nn.softmax(x, axis=axis)

def _gelu(x):
    return jax.nn.gelu(x, approximate=True)

def _silu(x):
    return jax.nn.silu(x)

def _sigmoid(x):
    return jax.nn.sigmoid(x)

def _layernorm(x, axis=-1, eps=1e-05):
    m = jnp.mean(x, axis=axis, keepdims=True)
    v = jnp.var(x, axis=axis, keepdims=True)
    return (x - m) / jnp.sqrt(v + eps)

def _scatter_add(tgt, idx, src, axis=0):
    return tgt.at[idx].add(src)

def _segment_sum(src, seg, n):
    return jax.ops.segment_sum(src, seg, n)
kernel_name = 'mk_xattn_seq_d4_seqx_r8_f09fc5'

def setup_inputs(seed: int=0):
    np.random.seed(seed)
    _w = jnp.asarray

    def _rec_inputs():
        import jax
        import jax.numpy as jnp
        _rk = jax.random.key(seed)
        x = -0.0002928 + 1 * jax.random.normal(jax.random.fold_in(_rk, 1), (8, 100, 128), jnp.float32)
        _lenS = 100 - jax.random.randint(jax.random.fold_in(_rk, 7), (8,), 0, max(1, 100 // 4) + 1, jnp.int32)
        _lenS2 = 1444 - jax.random.randint(jax.random.fold_in(_rk, 8), (8,), 0, max(1, 1444 // 4) + 1, jnp.int32)
        _ctx_768P = jax.random.normal(jax.random.fold_in(_rk, 11), (8, 16, 96), jnp.float32)
        _ctx_768c = jax.random.dirichlet(jax.random.fold_in(_rk, 511), 0.3 * jnp.ones((16,), jnp.float32), (8, 1444))
        _ctx_768t = jnp.einsum('bsk,bkd->bsd', _ctx_768c, _ctx_768P)
        _ctx_768t = _ctx_768t * jax.lax.rsqrt(jnp.mean(jnp.square(_ctx_768t)) + 1e-12) * 0.953939
        ctx_768 = -0.00055796 + 0.999787 * (_ctx_768t + 0.3 * jax.random.normal(jax.random.fold_in(_rk, 611), (8, 1444, 96), jnp.float32))
        _validS = jnp.arange(100)[None, :] < _lenS[:, None]
        _validS2 = jnp.arange(1444)[None, :] < _lenS2[:, None]
        _causal = jnp.tril(jnp.ones((100, 100), dtype=bool))
        mask_BxS_bf0 = jnp.logical_not(jnp.ones((8, 100), dtype=bool))
        mask_BxS2_bf0 = jnp.logical_not(jnp.ones((8, 1444), dtype=bool))
        return (x, ctx_768, mask_BxS_bf0, mask_BxS2_bf0)
    x, ctx_768, mask_BxS_bf0, mask_BxS2_bf0 = _rec_inputs()

    def _L0_xattn_setup():
        import jax, jax.numpy as jnp
        import numpy as np
        DIM = 128
        CTX_DIM = 96
        HEADS = 16
        HEAD_DIM = DIM // HEADS
        key = jax.random.key(seed)
        ks = jax.random.split(key, 8)
        B, L, Lc = (2, 256, 128)
        x = jax.random.normal(ks[0], (B, L, DIM), dtype=jnp.float32)
        context = jax.random.normal(ks[1], (B, Lc, CTX_DIM), dtype=jnp.float32)
        Wq = jax.random.normal(ks[2], (DIM, DIM), dtype=jnp.float32) * (1.0 / np.sqrt(DIM))
        Wk = jax.random.normal(ks[3], (DIM, CTX_DIM), dtype=jnp.float32) * (1.0 / np.sqrt(CTX_DIM))
        Wv = jax.random.normal(ks[4], (DIM, CTX_DIM), dtype=jnp.float32) * (1.0 / np.sqrt(CTX_DIM))
        Wo = jax.random.normal(ks[5], (DIM, DIM), dtype=jnp.float32) * (1.0 / np.sqrt(DIM))
        bo = jax.random.normal(ks[6], (DIM,), dtype=jnp.float32) * 0.01
        return {'x': x, 'context': context, 'Wq': Wq, 'Wk': Wk, 'Wv': Wv, 'Wo': Wo, 'bo': bo}
    _L0_xattn_all = _L0_xattn_setup()
    _L0_xattn_in = {k: v for k, v in _L0_xattn_all.items() if k in ('Wq', 'Wk', 'Wv', 'Wo', 'bo')}
    del _L0_xattn_all

    def _L1_xattn_setup():
        import jax, jax.numpy as jnp
        import numpy as np
        DIM = 128
        HEADS = 16
        D_HEAD = 64
        INNER = HEADS * D_HEAD
        CTX_DIM = 96
        FF_INNER = 4 * DIM
        EPS = 1e-05
        SCALE = D_HEAD ** (-0.5)

        def _layer_norm(x, g, b):
            m = jnp.mean(x, axis=-1, keepdims=True)
            v = jnp.mean(jnp.square(x - m), axis=-1, keepdims=True)
            return (x - m) * jax.lax.rsqrt(v + EPS) * g + b

        def _attention(x, ctx, wq, wk, wv, wo, bo):
            B, S, _ = x.shape
            T = ctx.shape[1]
            q = (x @ wq).reshape(B, S, HEADS, D_HEAD).transpose(0, 2, 1, 3)
            k = (ctx @ wk).reshape(B, T, HEADS, D_HEAD).transpose(0, 2, 1, 3)
            v = (ctx @ wv).reshape(B, T, HEADS, D_HEAD).transpose(0, 2, 1, 3)
            attn = jnp.einsum('bhid,bhjd->bhij', q, k) * SCALE
            attn = jax.nn.softmax(attn, axis=-1)
            out = jnp.einsum('bhij,bhjd->bhid', attn, v)
            out = out.transpose(0, 2, 1, 3).reshape(B, S, INNER)
            return out @ wo + bo
        key = jax.random.key(seed)
        ks = jax.random.split(key, 20)
        rn = lambda k, shape, s=0.02: jax.random.normal(k, shape, dtype=jnp.float32) * s
        inp = {'hidden_states': jax.random.normal(ks[0], (4, 256, DIM), dtype=jnp.float32), 'context': jax.random.normal(ks[1], (4, 77, CTX_DIM), dtype=jnp.float32), 'wq1': rn(ks[2], (DIM, INNER)), 'wk1': rn(ks[3], (DIM, INNER)), 'wv1': rn(ks[4], (DIM, INNER)), 'wo1': rn(ks[5], (INNER, DIM)), 'bo1': jnp.zeros((DIM,), jnp.float32), 'wq2': rn(ks[6], (DIM, INNER)), 'wk2': rn(ks[7], (CTX_DIM, INNER)), 'wv2': rn(ks[8], (CTX_DIM, INNER)), 'wo2': rn(ks[9], (INNER, DIM)), 'bo2': jnp.zeros((DIM,), jnp.float32), 'w_ff1': rn(ks[10], (DIM, 2 * FF_INNER)), 'b_ff1': jnp.zeros((2 * FF_INNER,), jnp.float32), 'w_ff2': rn(ks[11], (FF_INNER, DIM)), 'b_ff2': jnp.zeros((DIM,), jnp.float32), 'ln1_g': jnp.ones((DIM,), jnp.float32), 'ln1_b': jnp.zeros((DIM,), jnp.float32), 'ln2_g': jnp.ones((DIM,), jnp.float32), 'ln2_b': jnp.zeros((DIM,), jnp.float32), 'ln3_g': jnp.ones((DIM,), jnp.float32), 'ln3_b': jnp.zeros((DIM,), jnp.float32)}
        return inp
    _L1_xattn_all = _L1_xattn_setup()
    _L1_xattn_in = {k: v for k, v in _L1_xattn_all.items() if k in ('wq1', 'wk1', 'wv1', 'wo1', 'bo1', 'wq2', 'wk2', 'wv2', 'wo2', 'bo2', 'w_ff1', 'b_ff1', 'w_ff2', 'b_ff2', 'ln1_g', 'ln1_b', 'ln2_g', 'ln2_b', 'ln3_g', 'ln3_b')}
    del _L1_xattn_all

    def _L2_xattn_setup():
        import jax, jax.numpy as jnp
        import numpy as np
        import math
        N_HEADS = 16
        D_EMBED = 128
        D_CROSS = 96
        FF_DIM = 512
        D_HEAD = D_EMBED // N_HEADS
        LN_EPS = 1e-05

        def layer_norm(h, g, b):
            mu = jnp.mean(h, axis=-1, keepdims=True)
            var = jnp.var(h, axis=-1, keepdims=True)
            return (h - mu) * jax.lax.rsqrt(var + LN_EPS) * g + b

        def mha(q, k, v):
            B, Sq, _ = q.shape
            Skv = k.shape[1]
            qh = q.reshape(B, Sq, N_HEADS, D_HEAD).transpose(0, 2, 1, 3)
            kh = k.reshape(B, Skv, N_HEADS, D_HEAD).transpose(0, 2, 1, 3)
            vh = v.reshape(B, Skv, N_HEADS, D_HEAD).transpose(0, 2, 1, 3)
            scores = jnp.einsum('bhqd,bhkd->bhqk', qh, kh) / math.sqrt(D_HEAD)
            attn = jax.nn.softmax(scores, axis=-1)
            out = jnp.einsum('bhqk,bhkd->bhqd', attn, vh)
            return out.transpose(0, 2, 1, 3).reshape(B, Sq, D_EMBED)
        key = jax.random.key(seed)
        ks = jax.random.split(key, 24)
        s = 0.02
        inp = {'x': jax.random.normal(ks[0], (4, 128, D_EMBED), jnp.float32), 'y': jax.random.normal(ks[1], (4, 77, D_CROSS), jnp.float32), 'w_qkv': jax.random.normal(ks[2], (D_EMBED, 3 * D_EMBED), jnp.float32) * s, 'b_qkv': jnp.zeros((3 * D_EMBED,), jnp.float32), 'w_so': jax.random.normal(ks[3], (D_EMBED, D_EMBED), jnp.float32) * s, 'b_so': jnp.zeros((D_EMBED,), jnp.float32), 'w_q': jax.random.normal(ks[4], (D_EMBED, D_EMBED), jnp.float32) * s, 'b_q': jnp.zeros((D_EMBED,), jnp.float32), 'w_k': jax.random.normal(ks[5], (D_CROSS, D_EMBED), jnp.float32) * s, 'b_k': jnp.zeros((D_EMBED,), jnp.float32), 'w_v': jax.random.normal(ks[6], (D_CROSS, D_EMBED), jnp.float32) * s, 'b_v': jnp.zeros((D_EMBED,), jnp.float32), 'w_co': jax.random.normal(ks[7], (D_EMBED, D_EMBED), jnp.float32) * s, 'b_co': jnp.zeros((D_EMBED,), jnp.float32), 'w1': jax.random.normal(ks[8], (D_EMBED, FF_DIM), jnp.float32) * s, 'b1': jnp.zeros((FF_DIM,), jnp.float32), 'w2': jax.random.normal(ks[9], (FF_DIM, FF_DIM), jnp.float32) * s, 'b2': jnp.zeros((FF_DIM,), jnp.float32), 'w3': jax.random.normal(ks[10], (FF_DIM, D_EMBED), jnp.float32) * s, 'b3': jnp.zeros((D_EMBED,), jnp.float32), 'ln_g': jnp.ones((D_EMBED,), jnp.float32), 'ln_b': jnp.zeros((D_EMBED,), jnp.float32)}
        return inp
    _L2_xattn_all = _L2_xattn_setup()
    _L2_xattn_in = {k: v for k, v in _L2_xattn_all.items() if k in ('w_qkv', 'b_qkv', 'w_so', 'b_so', 'w_q', 'b_q', 'w_k', 'b_k', 'w_v', 'b_v', 'w_co', 'b_co', 'w1', 'b1', 'w2', 'b2', 'w3', 'b3', 'ln_g', 'ln_b')}
    del _L2_xattn_all

    def _L3_xattn_setup():
        import jax, jax.numpy as jnp
        import numpy as np
        D_DEC, D_ENC, H, D_MLP = (128, 96, 16, 512)
        HD = D_DEC // H

        def _layernorm(x, w, b, eps=1e-05):
            m = x.mean(-1, keepdims=True)
            v = ((x - m) ** 2).mean(-1, keepdims=True)
            return (x - m) / jnp.sqrt(v + eps) * w + b

        def _decoder_block(x, enc, tgt_mask, enc_mask, ln1_w, ln1_b, qkv_w, qkv_b, proj_w, proj_b, ln2_w, ln2_b, q_w, q_b, k_w, k_b, v_w, v_b, out_w, out_b, ln3_w, ln3_b, mlp1_w, mlp1_b, mlp2_w, mlp2_b):
            B, T, C = x.shape
            S = enc.shape[1]
            scale = HD ** (-0.5)
            neg = jnp.asarray(-jnp.inf, x.dtype)
            h = _layernorm(x, ln1_w, ln1_b)
            qkv = (h @ qkv_w + qkv_b).reshape(B, T, 3, H, HD)
            q, k, v = [qkv[:, :, i].transpose(0, 2, 1, 3) for i in range(3)]
            attn = jnp.einsum('bhtd,bhsd->bhts', q, k) * scale
            causal = jnp.triu(jnp.ones((T, T), bool), 1)
            attn = jnp.where(causal[None, None], neg, attn)
            attn = jnp.where(tgt_mask[:, None, None, :], neg, attn)
            attn = jax.nn.softmax(attn, axis=-1)
            sa = jnp.einsum('bhts,bhsd->bhtd', attn, v).transpose(0, 2, 1, 3).reshape(B, T, C)
            x = x + sa @ proj_w + proj_b
            h = _layernorm(x, ln2_w, ln2_b)
            q = (h @ q_w + q_b).reshape(B, T, H, HD).transpose(0, 2, 1, 3)
            k = (enc @ k_w + k_b).reshape(B, S, H, HD).transpose(0, 2, 1, 3)
            v = (enc @ v_w + v_b).reshape(B, S, H, HD).transpose(0, 2, 1, 3)
            attn = jnp.einsum('bhtd,bhsd->bhts', q, k) * scale
            attn = jnp.where(enc_mask[:, None, None, :], neg, attn)
            attn = jax.nn.softmax(attn, axis=-1)
            ca = jnp.einsum('bhts,bhsd->bhtd', attn, v).transpose(0, 2, 1, 3).reshape(B, T, C)
            x = x + ca @ out_w + out_b
            h = _layernorm(x, ln3_w, ln3_b)
            h = jax.nn.gelu(h @ mlp1_w + mlp1_b, approximate=False)
            x = x + h @ mlp2_w + mlp2_b
            return x
        key = jax.random.key(seed)
        ks = jax.random.split(key, 16)
        B, T, S = (4, 128, 72)

        def lin(k, din, dout):
            kw, kb = jax.random.split(k)
            bound = 1.0 / np.sqrt(din)
            W = jax.random.uniform(kw, (din, dout), jnp.float32, -bound, bound)
            b = jax.random.uniform(kb, (dout,), jnp.float32, -bound, bound)
            return (W, b)
        qkv_w, qkv_b = lin(ks[0], D_DEC, 3 * D_DEC)
        proj_w, proj_b = lin(ks[1], D_DEC, D_DEC)
        q_w, q_b = lin(ks[2], D_DEC, D_DEC)
        k_w, k_b = lin(ks[3], D_ENC, D_DEC)
        v_w, v_b = lin(ks[4], D_ENC, D_DEC)
        out_w, out_b = lin(ks[5], D_DEC, D_DEC)
        mlp1_w, mlp1_b = lin(ks[6], D_DEC, D_MLP)
        mlp2_w, mlp2_b = lin(ks[7], D_MLP, D_DEC)
        return {'x': jax.random.normal(ks[8], (B, T, D_DEC), jnp.float32), 'enc': jax.random.normal(ks[9], (B, S, D_ENC), jnp.float32), 'tgt_key_padding_mask': jnp.zeros((B, T), bool), 'enc_padding_mask': jnp.zeros((B, S), bool), 'ln1_w': jnp.ones((D_DEC,)), 'ln1_b': jnp.zeros((D_DEC,)), 'qkv_w': qkv_w, 'qkv_b': qkv_b, 'proj_w': proj_w, 'proj_b': proj_b, 'ln2_w': jnp.ones((D_DEC,)), 'ln2_b': jnp.zeros((D_DEC,)), 'q_w': q_w, 'q_b': q_b, 'k_w': k_w, 'k_b': k_b, 'v_w': v_w, 'v_b': v_b, 'out_w': out_w, 'out_b': out_b, 'ln3_w': jnp.ones((D_DEC,)), 'ln3_b': jnp.zeros((D_DEC,)), 'mlp1_w': mlp1_w, 'mlp1_b': mlp1_b, 'mlp2_w': mlp2_w, 'mlp2_b': mlp2_b}
    _L3_xattn_all = _L3_xattn_setup()
    _L3_xattn_in = {k: v for k, v in _L3_xattn_all.items() if k in ('ln1_w', 'ln1_b', 'qkv_w', 'qkv_b', 'proj_w', 'proj_b', 'ln2_w', 'ln2_b', 'q_w', 'q_b', 'k_w', 'k_b', 'v_w', 'v_b', 'out_w', 'out_b', 'ln3_w', 'ln3_b', 'mlp1_w', 'mlp1_b', 'mlp2_w', 'mlp2_b')}
    del _L3_xattn_all
    return {'x': x, 'ctx_768': ctx_768, 'mask_BxS_bf0': mask_BxS_bf0, 'mask_BxS2_bf0': mask_BxS2_bf0, 'L0_xattn_Wq': _L0_xattn_in['Wq'], 'L0_xattn_Wk': _L0_xattn_in['Wk'], 'L0_xattn_Wv': _L0_xattn_in['Wv'], 'L0_xattn_Wo': _L0_xattn_in['Wo'], 'L0_xattn_bo': _L0_xattn_in['bo'], 'L1_xattn_wq1': _L1_xattn_in['wq1'], 'L1_xattn_wk1': _L1_xattn_in['wk1'], 'L1_xattn_wv1': _L1_xattn_in['wv1'], 'L1_xattn_wo1': _L1_xattn_in['wo1'], 'L1_xattn_bo1': _L1_xattn_in['bo1'], 'L1_xattn_wq2': _L1_xattn_in['wq2'], 'L1_xattn_wk2': _L1_xattn_in['wk2'], 'L1_xattn_wv2': _L1_xattn_in['wv2'], 'L1_xattn_wo2': _L1_xattn_in['wo2'], 'L1_xattn_bo2': _L1_xattn_in['bo2'], 'L1_xattn_w_ff1': _L1_xattn_in['w_ff1'], 'L1_xattn_b_ff1': _L1_xattn_in['b_ff1'], 'L1_xattn_w_ff2': _L1_xattn_in['w_ff2'], 'L1_xattn_b_ff2': _L1_xattn_in['b_ff2'], 'L1_xattn_ln1_g': _L1_xattn_in['ln1_g'], 'L1_xattn_ln1_b': _L1_xattn_in['ln1_b'], 'L1_xattn_ln2_g': _L1_xattn_in['ln2_g'], 'L1_xattn_ln2_b': _L1_xattn_in['ln2_b'], 'L1_xattn_ln3_g': _L1_xattn_in['ln3_g'], 'L1_xattn_ln3_b': _L1_xattn_in['ln3_b'], 'L2_xattn_w_qkv': _L2_xattn_in['w_qkv'], 'L2_xattn_b_qkv': _L2_xattn_in['b_qkv'], 'L2_xattn_w_so': _L2_xattn_in['w_so'], 'L2_xattn_b_so': _L2_xattn_in['b_so'], 'L2_xattn_w_q': _L2_xattn_in['w_q'], 'L2_xattn_b_q': _L2_xattn_in['b_q'], 'L2_xattn_w_k': _L2_xattn_in['w_k'], 'L2_xattn_b_k': _L2_xattn_in['b_k'], 'L2_xattn_w_v': _L2_xattn_in['w_v'], 'L2_xattn_b_v': _L2_xattn_in['b_v'], 'L2_xattn_w_co': _L2_xattn_in['w_co'], 'L2_xattn_b_co': _L2_xattn_in['b_co'], 'L2_xattn_w1': _L2_xattn_in['w1'], 'L2_xattn_b1': _L2_xattn_in['b1'], 'L2_xattn_w2': _L2_xattn_in['w2'], 'L2_xattn_b2': _L2_xattn_in['b2'], 'L2_xattn_w3': _L2_xattn_in['w3'], 'L2_xattn_b3': _L2_xattn_in['b3'], 'L2_xattn_ln_g': _L2_xattn_in['ln_g'], 'L2_xattn_ln_b': _L2_xattn_in['ln_b'], 'L3_xattn_ln1_w': _L3_xattn_in['ln1_w'], 'L3_xattn_ln1_b': _L3_xattn_in['ln1_b'], 'L3_xattn_qkv_w': _L3_xattn_in['qkv_w'], 'L3_xattn_qkv_b': _L3_xattn_in['qkv_b'], 'L3_xattn_proj_w': _L3_xattn_in['proj_w'], 'L3_xattn_proj_b': _L3_xattn_in['proj_b'], 'L3_xattn_ln2_w': _L3_xattn_in['ln2_w'], 'L3_xattn_ln2_b': _L3_xattn_in['ln2_b'], 'L3_xattn_q_w': _L3_xattn_in['q_w'], 'L3_xattn_q_b': _L3_xattn_in['q_b'], 'L3_xattn_k_w': _L3_xattn_in['k_w'], 'L3_xattn_k_b': _L3_xattn_in['k_b'], 'L3_xattn_v_w': _L3_xattn_in['v_w'], 'L3_xattn_v_b': _L3_xattn_in['v_b'], 'L3_xattn_out_w': _L3_xattn_in['out_w'], 'L3_xattn_out_b': _L3_xattn_in['out_b'], 'L3_xattn_ln3_w': _L3_xattn_in['ln3_w'], 'L3_xattn_ln3_b': _L3_xattn_in['ln3_b'], 'L3_xattn_mlp1_w': _L3_xattn_in['mlp1_w'], 'L3_xattn_mlp1_b': _L3_xattn_in['mlp1_b'], 'L3_xattn_mlp2_w': _L3_xattn_in['mlp2_w'], 'L3_xattn_mlp2_b': _L3_xattn_in['mlp2_b']}

def reference(x, ctx_768, mask_BxS_bf0, mask_BxS2_bf0, L0_xattn_Wq, L0_xattn_Wk, L0_xattn_Wv, L0_xattn_Wo, L0_xattn_bo, L1_xattn_wq1, L1_xattn_wk1, L1_xattn_wv1, L1_xattn_wo1, L1_xattn_bo1, L1_xattn_wq2, L1_xattn_wk2, L1_xattn_wv2, L1_xattn_wo2, L1_xattn_bo2, L1_xattn_w_ff1, L1_xattn_b_ff1, L1_xattn_w_ff2, L1_xattn_b_ff2, L1_xattn_ln1_g, L1_xattn_ln1_b, L1_xattn_ln2_g, L1_xattn_ln2_b, L1_xattn_ln3_g, L1_xattn_ln3_b, L2_xattn_w_qkv, L2_xattn_b_qkv, L2_xattn_w_so, L2_xattn_b_so, L2_xattn_w_q, L2_xattn_b_q, L2_xattn_w_k, L2_xattn_b_k, L2_xattn_w_v, L2_xattn_b_v, L2_xattn_w_co, L2_xattn_b_co, L2_xattn_w1, L2_xattn_b1, L2_xattn_w2, L2_xattn_b2, L2_xattn_w3, L2_xattn_b3, L2_xattn_ln_g, L2_xattn_ln_b, L3_xattn_ln1_w, L3_xattn_ln1_b, L3_xattn_qkv_w, L3_xattn_qkv_b, L3_xattn_proj_w, L3_xattn_proj_b, L3_xattn_ln2_w, L3_xattn_ln2_b, L3_xattn_q_w, L3_xattn_q_b, L3_xattn_k_w, L3_xattn_k_b, L3_xattn_v_w, L3_xattn_v_b, L3_xattn_out_w, L3_xattn_out_b, L3_xattn_ln3_w, L3_xattn_ln3_b, L3_xattn_mlp1_w, L3_xattn_mlp1_b, L3_xattn_mlp2_w, L3_xattn_mlp2_b):
    import jax
    import jax.numpy as jnp

    def _L0_xattn_ref(x, context, Wq, Wk, Wv, Wo, bo):
        import jax, jax.numpy as jnp
        import numpy as np
        DIM = 128
        CTX_DIM = 96
        HEADS = 16
        HEAD_DIM = DIM // HEADS
        B, L, D = x.shape
        scale = HEAD_DIM ** (-0.5)
        q = jnp.einsum('bld,ed->ble', x, Wq)
        k = jnp.einsum('bcd,ed->bce', context, Wk)
        v = jnp.einsum('bcd,ed->bce', context, Wv)
        q = q.reshape(B, L, HEADS, HEAD_DIM).transpose(0, 2, 1, 3)
        k = k.reshape(B, -1, HEADS, HEAD_DIM).transpose(0, 2, 1, 3)
        v = v.reshape(B, -1, HEADS, HEAD_DIM).transpose(0, 2, 1, 3)
        attn = jnp.einsum('bhqd,bhkd->bhqk', q, k) * scale
        attn = jax.nn.softmax(attn, axis=-1)
        out = jnp.einsum('bhqk,bhkd->bhqd', attn, v)
        out = out.transpose(0, 2, 1, 3).reshape(B, L, D)
        return jnp.einsum('bld,ed->ble', out, Wo) + bo + x

    def _L1_xattn_ref(hidden_states, context, wq1, wk1, wv1, wo1, bo1, wq2, wk2, wv2, wo2, bo2, w_ff1, b_ff1, w_ff2, b_ff2, ln1_g, ln1_b, ln2_g, ln2_b, ln3_g, ln3_b):
        import jax, jax.numpy as jnp
        import numpy as np
        DIM = 128
        HEADS = 16
        D_HEAD = 64
        INNER = HEADS * D_HEAD
        CTX_DIM = 96
        FF_INNER = 4 * DIM
        EPS = 1e-05
        SCALE = D_HEAD ** (-0.5)

        def _layer_norm(x, g, b):
            m = jnp.mean(x, axis=-1, keepdims=True)
            v = jnp.mean(jnp.square(x - m), axis=-1, keepdims=True)
            return (x - m) * jax.lax.rsqrt(v + EPS) * g + b

        def _attention(x, ctx, wq, wk, wv, wo, bo):
            B, S, _ = x.shape
            T = ctx.shape[1]
            q = (x @ wq).reshape(B, S, HEADS, D_HEAD).transpose(0, 2, 1, 3)
            k = (ctx @ wk).reshape(B, T, HEADS, D_HEAD).transpose(0, 2, 1, 3)
            v = (ctx @ wv).reshape(B, T, HEADS, D_HEAD).transpose(0, 2, 1, 3)
            attn = jnp.einsum('bhid,bhjd->bhij', q, k) * SCALE
            attn = jax.nn.softmax(attn, axis=-1)
            out = jnp.einsum('bhij,bhjd->bhid', attn, v)
            out = out.transpose(0, 2, 1, 3).reshape(B, S, INNER)
            return out @ wo + bo
        h = hidden_states
        h = h + _attention(_layer_norm(h, ln1_g, ln1_b), _layer_norm(h, ln1_g, ln1_b), wq1, wk1, wv1, wo1, bo1)
        h = h + _attention(_layer_norm(h, ln2_g, ln2_b), context, wq2, wk2, wv2, wo2, bo2)
        x = _layer_norm(h, ln3_g, ln3_b) @ w_ff1 + b_ff1
        lin, gate = jnp.split(x, 2, axis=2)
        h = h + lin * jax.nn.gelu(gate) @ w_ff2 + b_ff2
        return h

    def _L2_xattn_ref(x, y, w_qkv, b_qkv, w_so, b_so, w_q, b_q, w_k, b_k, w_v, b_v, w_co, b_co, w1, b1, w2, b2, w3, b3, ln_g, ln_b):
        import jax, jax.numpy as jnp
        import numpy as np
        import math
        N_HEADS = 16
        D_EMBED = 128
        D_CROSS = 96
        FF_DIM = 512
        D_HEAD = D_EMBED // N_HEADS
        LN_EPS = 1e-05

        def layer_norm(h, g, b):
            mu = jnp.mean(h, axis=-1, keepdims=True)
            var = jnp.var(h, axis=-1, keepdims=True)
            return (h - mu) * jax.lax.rsqrt(var + LN_EPS) * g + b

        def mha(q, k, v):
            B, Sq, _ = q.shape
            Skv = k.shape[1]
            qh = q.reshape(B, Sq, N_HEADS, D_HEAD).transpose(0, 2, 1, 3)
            kh = k.reshape(B, Skv, N_HEADS, D_HEAD).transpose(0, 2, 1, 3)
            vh = v.reshape(B, Skv, N_HEADS, D_HEAD).transpose(0, 2, 1, 3)
            scores = jnp.einsum('bhqd,bhkd->bhqk', qh, kh) / math.sqrt(D_HEAD)
            attn = jax.nn.softmax(scores, axis=-1)
            out = jnp.einsum('bhqk,bhkd->bhqd', attn, vh)
            return out.transpose(0, 2, 1, 3).reshape(B, Sq, D_EMBED)
        qkv = x @ w_qkv + b_qkv
        q, k, v = jnp.split(qkv, 3, axis=-1)
        sa = mha(q, k, v) @ w_so + b_so
        x = layer_norm(x + sa, ln_g, ln_b)
        qc = x @ w_q + b_q
        kc = y @ w_k + b_k
        vc = y @ w_v + b_v
        ca = mha(qc, kc, vc) @ w_co + b_co
        x = layer_norm(x + ca, ln_g, ln_b)
        h = jax.nn.relu(x @ w1 + b1)
        h = jax.nn.relu(h @ w2 + b2)
        ff = h @ w3 + b3
        x = layer_norm(x + ff, ln_g, ln_b)
        return x

    def _L3_xattn_ref(x, enc, tgt_key_padding_mask, enc_padding_mask, ln1_w, ln1_b, qkv_w, qkv_b, proj_w, proj_b, ln2_w, ln2_b, q_w, q_b, k_w, k_b, v_w, v_b, out_w, out_b, ln3_w, ln3_b, mlp1_w, mlp1_b, mlp2_w, mlp2_b):
        import jax, jax.numpy as jnp
        import numpy as np
        D_DEC, D_ENC, H, D_MLP = (128, 96, 16, 512)
        HD = D_DEC // H

        def _layernorm(x, w, b, eps=1e-05):
            m = x.mean(-1, keepdims=True)
            v = ((x - m) ** 2).mean(-1, keepdims=True)
            return (x - m) / jnp.sqrt(v + eps) * w + b

        def _decoder_block(x, enc, tgt_mask, enc_mask, ln1_w, ln1_b, qkv_w, qkv_b, proj_w, proj_b, ln2_w, ln2_b, q_w, q_b, k_w, k_b, v_w, v_b, out_w, out_b, ln3_w, ln3_b, mlp1_w, mlp1_b, mlp2_w, mlp2_b):
            B, T, C = x.shape
            S = enc.shape[1]
            scale = HD ** (-0.5)
            neg = jnp.asarray(-jnp.inf, x.dtype)
            h = _layernorm(x, ln1_w, ln1_b)
            qkv = (h @ qkv_w + qkv_b).reshape(B, T, 3, H, HD)
            q, k, v = [qkv[:, :, i].transpose(0, 2, 1, 3) for i in range(3)]
            attn = jnp.einsum('bhtd,bhsd->bhts', q, k) * scale
            causal = jnp.triu(jnp.ones((T, T), bool), 1)
            attn = jnp.where(causal[None, None], neg, attn)
            attn = jnp.where(tgt_mask[:, None, None, :], neg, attn)
            attn = jax.nn.softmax(attn, axis=-1)
            sa = jnp.einsum('bhts,bhsd->bhtd', attn, v).transpose(0, 2, 1, 3).reshape(B, T, C)
            x = x + sa @ proj_w + proj_b
            h = _layernorm(x, ln2_w, ln2_b)
            q = (h @ q_w + q_b).reshape(B, T, H, HD).transpose(0, 2, 1, 3)
            k = (enc @ k_w + k_b).reshape(B, S, H, HD).transpose(0, 2, 1, 3)
            v = (enc @ v_w + v_b).reshape(B, S, H, HD).transpose(0, 2, 1, 3)
            attn = jnp.einsum('bhtd,bhsd->bhts', q, k) * scale
            attn = jnp.where(enc_mask[:, None, None, :], neg, attn)
            attn = jax.nn.softmax(attn, axis=-1)
            ca = jnp.einsum('bhts,bhsd->bhtd', attn, v).transpose(0, 2, 1, 3).reshape(B, T, C)
            x = x + ca @ out_w + out_b
            h = _layernorm(x, ln3_w, ln3_b)
            h = jax.nn.gelu(h @ mlp1_w + mlp1_b, approximate=False)
            x = x + h @ mlp2_w + mlp2_b
            return x
        return _decoder_block(x, enc, tgt_key_padding_mask, enc_padding_mask, ln1_w, ln1_b, qkv_w, qkv_b, proj_w, proj_b, ln2_w, ln2_b, q_w, q_b, k_w, k_b, v_w, v_b, out_w, out_b, ln3_w, ln3_b, mlp1_w, mlp1_b, mlp2_w, mlp2_b)
    x = _L0_xattn_ref(x, ctx_768, L0_xattn_Wq, L0_xattn_Wk, L0_xattn_Wv, L0_xattn_Wo, L0_xattn_bo)
    x = _L1_xattn_ref(x, ctx_768, L1_xattn_wq1, L1_xattn_wk1, L1_xattn_wv1, L1_xattn_wo1, L1_xattn_bo1, L1_xattn_wq2, L1_xattn_wk2, L1_xattn_wv2, L1_xattn_wo2, L1_xattn_bo2, L1_xattn_w_ff1, L1_xattn_b_ff1, L1_xattn_w_ff2, L1_xattn_b_ff2, L1_xattn_ln1_g, L1_xattn_ln1_b, L1_xattn_ln2_g, L1_xattn_ln2_b, L1_xattn_ln3_g, L1_xattn_ln3_b)
    x = _L2_xattn_ref(x, ctx_768, L2_xattn_w_qkv, L2_xattn_b_qkv, L2_xattn_w_so, L2_xattn_b_so, L2_xattn_w_q, L2_xattn_b_q, L2_xattn_w_k, L2_xattn_b_k, L2_xattn_w_v, L2_xattn_b_v, L2_xattn_w_co, L2_xattn_b_co, L2_xattn_w1, L2_xattn_b1, L2_xattn_w2, L2_xattn_b2, L2_xattn_w3, L2_xattn_b3, L2_xattn_ln_g, L2_xattn_ln_b)
    x = _L3_xattn_ref(x, ctx_768, mask_BxS_bf0, mask_BxS2_bf0, L3_xattn_ln1_w, L3_xattn_ln1_b, L3_xattn_qkv_w, L3_xattn_qkv_b, L3_xattn_proj_w, L3_xattn_proj_b, L3_xattn_ln2_w, L3_xattn_ln2_b, L3_xattn_q_w, L3_xattn_q_b, L3_xattn_k_w, L3_xattn_k_b, L3_xattn_v_w, L3_xattn_v_b, L3_xattn_out_w, L3_xattn_out_b, L3_xattn_ln3_w, L3_xattn_ln3_b, L3_xattn_mlp1_w, L3_xattn_mlp1_b, L3_xattn_mlp2_w, L3_xattn_mlp2_b)
    return x

_drawn_inputs = setup_inputs


def setup_inputs(seed=0):
    import zlib

    import numpy as np

    out = dict(_drawn_inputs(seed))
    spreads = {'L1_xattn_bo1': (0.0, 0.1),
     'L1_xattn_bo2': (0.0, 0.1),
     'L1_xattn_b_ff1': (0.0, 0.8),
     'L1_xattn_b_ff2': (0.0, 0.358),
     'L1_xattn_ln1_g': (1.0, 0.6),
     'L1_xattn_ln1_b': (0.0, 0.72),
     'L1_xattn_ln2_g': (1.0, 0.6),
     'L1_xattn_ln2_b': (0.0, 0.8),
     'L1_xattn_ln3_g': (1.0, 0.6),
     'L1_xattn_ln3_b': (0.0, 0.8),
     'L2_xattn_b_qkv': (0.0, 1.566),
     'L2_xattn_b_so': (0.0, 0.309),
     'L2_xattn_b_q': (0.0, 0.8),
     'L2_xattn_b_k': (0.0, 2.0),
     'L2_xattn_b_v': (0.0, 0.499),
     'L2_xattn_b_co': (0.0, 0.1),
     'L2_xattn_b1': (0.0, 0.8),
     'L2_xattn_b2': (0.0, 0.397),
     'L2_xattn_b3': (0.0, 0.1),
     'L2_xattn_ln_g': (1.0, 0.2),
     'L2_xattn_ln_b': (0.0, 0.1),
     'L3_xattn_ln1_w': (1.0, 0.2),
     'L3_xattn_ln1_b': (0.0, 0.367),
     'L3_xattn_ln2_w': (1.0, 0.6),
     'L3_xattn_ln2_b': (0.0, 0.8),
     'L3_xattn_ln3_w': (1.0, 0.582),
     'L3_xattn_ln3_b': (0.0, 0.542)}
    factors = {'L0_xattn_bo': 7.32,
     'L1_xattn_wq1': 8.0,
     'L1_xattn_wk1': 8.0,
     'L1_xattn_wq2': 8.0,
     'L1_xattn_wk2': 8.0,
     'L1_xattn_w_ff1': 4.711,
     'L1_xattn_w_ff2': 4.71,
     'L2_xattn_w_q': 8.0,
     'L2_xattn_w_k': 8.0,
     'L2_xattn_w_v': 3.368,
     'L2_xattn_w1': 3.881,
     'L2_xattn_w2': 3.16,
     'L3_xattn_q_w': 3.442,
     'L3_xattn_q_b': 8.0,
     'L3_xattn_k_w': 3.413,
     'L3_xattn_k_b': 64.0,
     'L3_xattn_mlp1_b': 4.282,
     'L3_xattn_mlp2_b': 2.858}
    for name, (base, spread) in spreads.items():
        noise = np.random.default_rng([zlib.crc32(name.encode()), seed]).standard_normal(out[name].shape)
        drawn = base * np.exp(spread * noise) if base else spread * noise
        out[name] = jnp.asarray(drawn.astype(out[name].dtype))
    for name, factor in factors.items():
        out[name] = (out[name] * factor).astype(out[name].dtype)
    return out
```

```python
from contextlib import ExitStack

import concourse.bass as bass
from concourse import mybir

F32 = mybir.dt.float32
F32R = mybir.dt.float32r
U8 = mybir.dt.uint8
ALU = mybir.AluOpType
ACT = mybir.ActivationFunctionType
AX = mybir.AxisListType

B, S, D, H, T, C = 8, 100, 128, 16, 1444, 96
N = B * S
HALF = N // 2
NT = -(-T // 128)
TC = [128] * (NT - 2) + [(T - 128 * (NT - 2)) // 2] * 2
TO = [sum(TC[:c]) for c in range(NT)]
GQ = 4 * S
HQ = H * S
EPS = 1e-5
NEG = -1e30
D1 = 64
S8 = 8 ** -0.5
S64 = D1 ** -0.5
QT = -(-HQ // 128)
MC = [482, 482, 480]
UNITS = QT * len(MC)

BIAS = ["eps", "negsel", "bo0", "b1o1", "b1o2", "l1g1", "l1b1", "l1g2", "l1b2", "l1g3", "l1b3",
        *[f"bf1_{t}" for t in range(8)], "bf2",
        "b2q", "b2k", "b2so", "b2co", *[f"b21_{t}" for t in range(4)], *[f"b22_{t}" for t in range(4)], "b23",
        "l2g", "l2b", "l3g1", "l3b1", "b3q", "b3k", "b3p", "l3g2", "l3b2", "b3o", "l3g3", "l3b3",
        *[f"b31_{t}" for t in range(4)], "b32",
        *[f"qr{n}_{g}" for n in range(3) for g in range(4)]]
BI = {n: i for i, n in enumerate(BIAS)}

def offsets(parts):
    at, out = 0, {}
    for name, width in parts:
        out[name] = at
        at += width
    out["end"] = at
    return out

ATT8 = [("qr", 4 * 128), ("k", 128), ("v", 128), ("co", 4 * 128)]
SELF8 = [("sq", 128), ("sk", 128), ("sv", 128), ("bv", 128), ("so", 4 * 128)]
W0 = offsets(ATT8)
W2 = offsets(ATT8 + SELF8 + [("w1", 512), ("w2", 4 * 512), ("w3", 4 * 128)])
W3 = offsets(ATT8 + SELF8 + [("w1", 512), ("w3", 4 * 128)])
WOFF = [W0, W2, W3]
CONST = offsets([("ident", 128), ("mean", 128), ("sums", 4), ("mask4", 4), ("mask16", 16), ("left4", 4), ("left16", 16), ("causal", S)])


def build(nc, xT_d, ctxT_d, ctxN_d, w0_d, w2_d, w3_d, wf_d, ff1_d, ff2_d, bias_d, const_d, tmask_d, cmask_d, out_d):
    with ExitStack() as ctx:
        def sb(name, shape, dt=F32, scope=ctx):
            return scope.enter_context(nc.sbuf_tensor(name, shape, dt))

        names = {}

        def sem(name):
            if name not in names:
                names[name] = ctx.enter_context(nc.semaphore(name))
            return names[name]

        PS = ctx.enter_context(nc.psum_tensor("PS", [128, 8, 512], F32))

        x = sb("x", [128, N])
        YS = sb("YS", [128, 4, N])
        y, xc, sq = YS[:, 0, :], YS[:, 1, :], YS[:, 2, :]
        O8 = YS
        bias = sb("bias", [128, len(BIAS)])
        std, rstd = sb("std", [S, B]), sb("rstd", [S, B])
        const = sb("const", [128, CONST["end"]])
        PT = sb("PT", [128, 2, HQ])
        U = PT[:, :, :].rearrange("p a (b n) -> p (a b) n", b=2)
        qf = [U[:, 0, :], U[:, 1, :]]

        def bcol(name, rows=128):
            return bias[0:rows, BI[name]:BI[name] + 1]

        def cpart(name, width, rows=128):
            return const[0:rows, CONST[name]:CONST[name] + width]

        ident, meanw, sumrow = cpart("ident", 128), cpart("mean", 128), cpart("sums", 4)
        mask4, mask16, left4, left16, causal = cpart("mask4", 4), cpart("mask16", 16), cpart("left4", 4, 64), cpart("left16", 16, 64), cpart("causal", S, S)

        def self_buffers(tag, scope):
            shapes = dict(xq=[128, 2, S], qs=[128, 2, S], Kbd=[128, 2, H, S] if tag == "8" else [1, 1], Ps=[S, H, S] if tag == "8" else [1, 1], Pe=[S, 2, H, S], Pn=[S, H, S],
                          smx=[S, H], ssum=[S, H], srec=[S, H], Vn=[S, 2, 144])
            return {k: sb(k + tag, v, F32, scope) for k, v in shapes.items()}

        e8 = ExitStack()
        W = sb("W", [128, W2["end"]], F32, e8)
        e8c = ExitStack()
        Kcat = [sb(f"Kcat{p}", [128, 4, T], F32R, e8c) for p in range(3)]
        kh = sb("kh", [128, T], F32R, e8c)
        kl = sb("kl", [128, T], F32R, e8c)
        ctxT8 = sb("ctxT8", [C + 1, T], F32, e8c)
        VW = 8 * 17
        Vaug = [sb(f"Vaug{p}", [128, NT * VW + 16], F32, e8c) for p in range(3)]
        Qbd = [sb(f"Qbd{p}", [128, 4, GQ], F32R, e8c) for p in range(3)]
        QR = sb("QR", [128, 4, N], F32R, e8c)
        osb = sb("osb", [128, GQ], F32, e8c)
        Qleft = [sb(f"Qleft{p}", [128, 320], F32R, e8c) for p in range(3)]
        rec = sb("rec", [S, 4, 4], F32, e8c)
        mx8 = sb("mx8", [128, QT, 3], F32, e8c)
        nm8 = sb("nm8", [128, QT], F32, e8c)
        nmleft = sb("nmleft", [64, 4], F32, e8c)
        nmTh8 = sb("nmTh8", [4, GQ], F32R, e8c)
        nmTl8 = sb("nmTl8", [4, GQ], F32R, e8c)
        e8c.close()
        e8s = ExitStack()
        self8b = self_buffers("8", e8s)
        qT = sb("qT", [128, N], F32, e8s)
        kT = sb("kT", [128, N], F32, e8s)
        U2 = sb("U2", [128, 4, N], F32, e8s)
        cmb = sb("cmb", [S, B, S], F32, e8s)
        tmask = sb("tmask", [S, B, S], U8, e8s)
        e8s.close()
        e8.close()

        e1 = ExitStack()
        BIG = sb("BIG", [128, H, N], F32, e1)
        WB2 = sb("WB2", [128, H, 128], F32, e1)
        FF1 = sb("FF1", [128, 8 * 128], F32, e1)
        FF2 = sb("FF2", [128, 4 * 128], F32, e1)
        e1s = ExitStack()
        self1b = self_buffers("1", e1s)
        WA1 = sb("WA1", [128, H, 128], F32, e1s)
        WB1 = sb("WB1", [128, H, 128], F32, e1s)
        WF = sb("WF", [128, 8, 8, 128], F32, e1s)
        WA2 = sb("WA2", [128, H, 128], F32, e1s)
        e1s.close()
        e1c = ExitStack()
        raw1 = sb("raw1", [128, T], F32, e1c)
        ch = [sb(f"ch{p}", [C, T], F32R, e1c) for p in range(2)]
        cl = [sb(f"cl{p}", [C, T], F32R, e1c) for p in range(2)]
        nh = [sb(f"nh{p}", [128, NT, C], F32R, e1c) for p in range(2)]
        nl = [sb(f"nl{p}", [128, NT, C], F32R, e1c) for p in range(2)]
        Qh = sb("Qh", [C, 2, GQ], F32R, e1c)
        Ql = sb("Ql", [C, 2, GQ], F32R, e1c)
        P1 = sb("P1", [S, 2, 4, T], F32, e1c)
        Ph = sb("Ph", [128, 2, GQ], F32R, e1c)
        Pl = sb("Pl", [128, 2, GQ], F32R, e1c)
        ob1 = sb("ob1", [C, GQ], F32, e1c)
        mx1 = sb("mx1", [S, H, 3], F32, e1c)
        shift1 = sb("shift1", [S, H], F32, e1c)
        sums1 = sb("sums1", [S, H, 3], F32, e1c)
        sum1 = sb("sum1", [S, 4], F32, e1c)
        inv1 = sb("inv1", [S, 4], F32, e1c)
        e1c.close()
        e1.close()

        RATE = dict(
            ctx_loaded8=16, kcat_loaded=192, mrow_loaded8=32, mask_loaded=16,
            ctx_loaded1=16, cn_loaded=16,
            kproj=4, vproj=3, smax8=UNITS, nmT8=1, st8=4 * NT, pv8=NT, sums8=1, bcast8=1,
            scored1=3 * H, turned1=4 * NT, pv1=4 * NT, bcast1=4,
            self_scores=4, self_turned=1, self_pv=1,
            kh_done=4, v_copied=4, exp8=4 * NT, pv_copied8=1, exp1=3 * H, high1=4 * NT, pv_copied1=4,
            self_exp=4, self_pt=1, self_out64=1,
            kl_done=4, max_read8=UNITS, nm_ready8=2, nm_high8=1, nm_split8=1, rec8=1, on8=1,
            max_read1=3 * H, shift1=H, low1=4 * NT, sum1=4, rec1=4, on1=4,
            self_masked=4, self_max=4, self_rec=1, self_v=1, self_out8=1,
            qbd_built=5, ctx_split=2, cn_split=2, q_split=8, xq_copied=1, qs_copied=1, kbd_built=1, self_norm=1)
        OWNER = dict(
            sync="ctx_loaded8 kcat_loaded mrow_loaded8 ctx_loaded1 cn_loaded",
            tensor="kproj vproj smax8 nmT8 st8 pv8 sums8 bcast8 scored1 turned1 pv1 bcast1 self_scores self_turned self_pv",
            scalar="kh_done v_copied exp8 pv_copied8 exp1 high1 pv_copied1 self_exp self_pt",
            vector="kl_done max_read8 nm_ready8 nm_high8 nm_split8 rec8 on8 max_read1 shift1 low1 "
                   "sum1 rec1 on1 self_masked self_max self_rec self_v self_out8 self_out64",
            gpsimd="qbd_built ctx_split cn_split q_split xq_copied qs_copied kbd_built self_norm")

        def credit(eng, who):
            for name in OWNER[who].split():
                eng.sem_inc(sem(name), RATE[name])

        def wait(eng, name, g, k):
            eng.wait_ge(sem(name), RATE[name] * g + k)

        def settle(eng):
            eng.sem_inc(sem("steps_sync" if eng is nc.sync else "steps_gpsimd"), 1)

        def cols(b, w=S):
            return bass.ds(b * w, w)

        order = []
        order += [f"qr0_{g}" for g in range(4)] + ["proj0"]
        order += ["m0", "v0", "r0"] + [f"fuse{k}{t}" for k in "ABCD" for t in range(2)]
        order += [f"k64_{h}" for h in range(H)] + ["proj1"]
        order += ["m1", "v1", "r1"] + [f"q64_{h}" for h in range(H)] + ["proj2", "m2", "v2", "r2"]
        order += [f"{a}{t}" for t in range(4) for a in ("gate", "lin")] + ["ff2"]
        order += ["sq1", "sk1", "proj3", "m3", "v3", "r3"] + [f"qr1_{g}" for g in range(4)] + ["proj4", "m4", "v4", "r4"]
        order += [f"h1_{t}" for t in range(4)] + [f"h2_{t}" for t in range(4)] + ["h3", "m5", "v5", "r5"]
        order += ["m6", "v6", "r6", "sq2", "sk2", "proj5", "m7", "v7", "r7"] + [f"qr2_{g}" for g in range(4)]
        order += ["proj6", "m8", "v8", "r8"] + [f"g1_{t}" for t in range(4)] + ["g2"]
        TI = {name: i for i, name in enumerate(order)}

        def tile(name, width=HALF, rows=128):
            k = TI[name] % 2
            return PS[0:rows, 2 * k:2 * k + 2, 0:width]

        def tile_free(pe, name):
            if TI[name] >= 2:
                pe.wait_ge(sem(f"tile_taken{TI[name] % 2}"), TI[name] // 2)

        def tile_full(eng, name):
            eng.wait_ge(sem("tile_full"), TI[name] + 1)

        def taken(ins, name):
            return ins.then_inc(sem(f"tile_taken{TI[name] % 2}"), 1)

        def gone(eng, *names):
            for name in names:
                eng.wait_ge(sem(f"tile_taken{TI[name] % 2}"), TI[name] // 2 + 1)

        X_BY = ["proj0", "proj1", "proj2", "ff2", "proj3", None, "proj4", None, "h3", None, "proj5", "proj6", "g2"]

        def x_ready(eng, count):
            name = X_BY[count - 1]
            if name:
                gone(eng, name)
            else:
                eng.wait_ge(sem("x_normed"), X_BY[:count].count(None))

        def halves(ap):
            return ap.rearrange("p (a n) -> p a n", a=2)

        def dense(pe, name, terms, rows=128):
            tile_free(pe, name)
            out = tile(name, rows=rows)
            for a in range(2):
                for i, (lhsT, rhs) in enumerate(terms):
                    last = pe.matmul(out[:, a, :], lhsT, rhs[:, a * HALF:(a + 1) * HALF],
                                     start=(i == 0), stop=(i == len(terms) - 1))
            last.then_inc(sem("tile_full"), 1)

        def wcol(n, name, i, rows=128):
            return W[0:rows, WOFF[n][name] + 128 * i:WOFF[n][name] + 128 * (i + 1)]

        def ln_pe(pe, k, src, n=None):
            x_ready(pe, XN[k])
            dense(pe, f"m{k}", [(meanw, src)])
            prep0(pe, n, 0)
            pe.wait_ge(sem("ln_sq"), k + 1)
            tile_free(pe, f"v{k}")
            for b in range(B):
                last = pe.matmul(tile(f"v{k}")[0:S, 0, b:b + 1], sq[:, S * b:S * b + S], meanw[:, 0:1], start=True, stop=True)
            last.then_inc(sem("tile_full"), 1)
            prep0(pe, n, 1)
            tile_free(pe, f"r{k}")
            pe.wait_ge(sem("ln_rec"), k + 1)
            for b in range(B):
                last = pe.matmul(tile(f"r{k}")[:, b // 4, S * (b % 4):S * (b % 4) + S],
                                 rstd[:, b:b + 1].broadcast_to([S, 128]), ident[0:S, 0:S], start=True, stop=True)
            last.then_inc(sem("tile_full"), 1)
            prep0(pe, n, 2)

        def ln_act(act, k, n=None):
            gone(act, f"m{k}")
            act.activation(sq, xc, ACT.Square).then_inc(sem("ln_sq"), 1)
            prep0(act, n, 0)
            tile_full(act, f"v{k}")
            taken(act.activation(std[:, :], tile(f"v{k}")[0:S, 0, 0:B], ACT.Sqrt, bias=bcol("eps", S)), f"v{k}")
            prep0(act, n, 1)
            prep0(act, n, 2)

        def ln_dve(dve, k, src, dst, g, b, done, n=None):
            tile_full(dve, f"m{k}")
            taken(dve.tensor_tensor(halves(xc), halves(src), tile(f"m{k}"), ALU.subtract), f"m{k}")
            prep0(dve, n, 0)
            gone(dve, f"v{k}")
            dve.reciprocal(rstd[:, :], std[:, :]).then_inc(sem("ln_rec"), 1)
            prep0(dve, n, 1)
            tile_full(dve, f"r{k}")
            gone(dve, f"m{k}")
            taken(dve.tensor_tensor(halves(xc), halves(xc), tile(f"r{k}"), ALU.mult), f"r{k}")
            gone(dve, f"r{k}")
            dve.tensor_scalar(dst, xc, bcol(g), bcol(b), ALU.mult, ALU.add).then_inc(sem(done), 1)
            prep0(dve, n, 2)

        XN = {0: 1, 1: 2, 2: 3, 3: 5, 4: 7, 5: 9, 6: 10, 7: 11, 8: 12}

        def add_to_x(dve, name, b, self_wait):
            tile_full(dve, name)
            if self_wait:
                x_ready(dve, self_wait)
            taken(dve.scalar_tensor_tensor(halves(x[:, :]), tile(name), bcol(b), halves(x[:, :]), ALU.add, ALU.add),
                  name)

        def qr_pe(pe, n, src):
            for g in range(4):
                dense(pe, f"qr{n}_{g}", [(wcol(n, "qr", g), src)])
                prep0(pe, n, 3 + g)

        def qr_act(act, n):
            for g in range(4):
                tile_full(act, f"qr{n}_{g}")
                if 4 * n + g >= 2:
                    act.wait_ge(sem("qr_split"), 4 * n + g - 1)
                taken(act.activation(halves(qf[g % 2]), tile(f"qr{n}_{g}"), ACT.Identity, bias=bcol(f"qr{n}_{g}")),
                      f"qr{n}_{g}")
                prep0(act, n, 3 + g)

        def qr_dve(dve, n):
            for g in range(4):
                gone(dve, f"qr{n}_{g}")
                dve.tensor_copy(QR[:, g, :], qf[g % 2]).then_inc(sem("qr_high"), 1)
                dve.wait_ge(sem("qr_high"), 4 * n + g + 1)
                dve.scalar_tensor_tensor(QR[:, g, :], QR[:, g, :].bitcast(F32), bcol("negsel"), qf[g % 2],
                                         ALU.mult, ALU.add).then_inc(sem("qr_split"), 1)
                prep0(dve, n, 3 + g)

        HEAD = 9
        KP = [3, 7, 11, 15]
        VP = [19, 23, 27]
        TURN = UNITS - HEAD + 3
        ST_STEPS = 33
        RECIP = ST_STEPS + 4
        TH = T // 4

        def st_of(s):
            return range(min(48, -(-48 * s // ST_STEPS)), min(48, -(-48 * (s + 1) // ST_STEPS)))

        def units(s, gm, gp, pm, pp, prep, mxs):
            if s < UNITS - HEAD:
                return [(s + HEAD, gm, pm)] if mxs else []
            return [(s + HEAD - UNITS, gp, pp)] if prep else []

        def tile_rows(t):
            return min(128, HQ - 128 * t)

        def pe_unit8(pe, n, u, g, r, first, second):
            t, k = u // 3, u % 3
            wait(pe, "max_read8", g, u - 2)
            if u == 0:
                wait(pe, "qbd_built", g, 5)
                wait(pe, "kcat_loaded", g, 192)
                if first:
                    pe.wait_ge(sem("ones_k"), 2 * (n + 1))
                elif second:
                    pe.wait_ge(sem("ones_k2"), 2 * (n + 1))
                if n == 2:
                    wait(pe, "mask_loaded", g - 2 * B, 0)
            part = slice(482 * k, 482 * k + MC[k])
            out = PS[0:tile_rows(t), u % 3, 0:MC[k]]
            if t < QT - 1:
                q0 = 128 * (t % 3)
                last = pe.matmul(out, Qbd[r][:, t // 3, q0:q0 + 128], Kcat[r][:, t // 3, part], start=True, stop=True)
            else:
                for a in range(4):
                    last = pe.matmul(out, Qleft[r][:, 64 * a:64 * a + 64], Kcat[r][:, a, part],
                                     start=(a == 0), stop=(a == 3))
            last.then_inc(sem("smax8"), 1)

        def pe_key(pe, n, gp, k, bank):
            wait(pe, "kl_done", gp, k) if k else wait(pe, "ctx_loaded8", gp, 16)
            pe.matmul(PS[:, bank, 0:TH], wcol(n, "k", 0, C + 1), ctxT8[:, TH * k:TH * (k + 1)],
                      start=True, stop=True).then_inc(sem("kproj"), 1)

        def act_key(act, gp, k, bank):
            wait(act, "kproj", gp, k + 1)
            wait(act, "kcat_loaded", gp, 0)
            act.activation(kh[:, TH * k:TH * (k + 1)], PS[:, bank, 0:TH], ACT.Copy).then_inc(sem("kh_done"), 1)

        def dve_key(dve, gp, k, bank):
            part = slice(TH * k, TH * (k + 1))
            wait(dve, "kh_done", gp, k + 1)
            dve.tensor_tensor(kl[:, part], PS[:, bank, 0:TH], kh[:, part].bitcast(F32), ALU.subtract)\
               .then_inc(sem("kl_done"), 1)

        def pe_value(pe, n, gp, k, bank):
            wait(pe, "v_copied", gp, k) if k else wait(pe, "kl_done", gp, 4)
            for j in range(4):
                t = 4 * k + j
                last = pe.matmul(PS[0:TC[t], bank, 128 * j:128 * j + 128], ctxT8[:, TO[t]:TO[t] + TC[t]],
                                 wcol(n, "v", 0, C + 1), start=True, stop=True)
            last.then_inc(sem("vproj"), 1)

        def act_value(act, gp, pp, k, bank):
            v = Vaug[pp][:, 0:NT * VW].rearrange("p (a e) -> p a e", e=17)
            wait(act, "vproj", gp, k + 1)
            for lo, hi, rows in ((0, 32, 128),) if k < 2 else ((0, 16, 128), (16, 32, TC[-1])):
                act.activation(v[0:rows, 32 * k + lo:32 * k + hi, 0:16],
                               PS[0:rows, bank, 16 * lo:16 * hi].rearrange("p (a e) -> p a e", e=16),
                               ACT.Copy).then_inc(sem("v_copied"), 1)

        def prep0(eng, n, j):
            if n is None:
                return
            gp = 1 + B * n
            if eng is nc.tensor:
                pe_key(eng, n, gp, j, 7) if j < 4 else pe_value(eng, n, gp, j - 4, 7)
            elif eng is nc.scalar:
                if j < 4:
                    act_key(eng, gp, j, 7)
                else:
                    if j == 4:
                        eng.wait_ge(sem("ones_v"), 3 * (n + 1))
                    act_value(eng, gp, 0, j - 4, 7)
            elif j < 4:
                dve_key(eng, gp, j, 7)

        def pe_iter8(pe, n, i, r, prep, mxs, out):
            gp, gm, go = 2 + B * n + i, 1 + B * n + i, B * n + i
            pp, pm, po = (r + 1) % 3, r, (r - 1) % 3
            peeled = isinstance(i, int)
            if out:
                wait(pe, "mrow_loaded8", go, 32)
            for s in range(UNITS):
                if prep and s in KP and not (peeled and i == -1):
                    k = KP.index(s)
                    if k == 0:
                        wait(pe, "v_copied", gp, 0)
                        wait(pe, "nm_split8", gm, 0)
                        if not peeled:
                            wait(pe, "on8", go, 0)
                    pe_key(pe, n, gp, k, 3)
                if prep and s in VP and not (peeled and i == -1):
                    pe_value(pe, n, gp, VP.index(s), 3)
                if mxs and s == TURN:
                    wait(pe, "nm_ready8", gm, 2)
                    if prep:
                        wait(pe, "v_copied", gp, 4)
                    if out:
                        wait(pe, "on8", go, 0)
                    for j in range(3):
                        pe.transpose(PS[0:4, 3, 128 * j:128 * j + 128], nm8[:, j:12:3], ident)
                    pe.matmul(PS[0:4, 3, 384:GQ], nmleft[:, :], left16, start=True, stop=True).then_inc(sem("nmT8"), 1)
                for u, g, ru in units(s, gm, gp, pm, pp, prep, mxs):
                    pe_unit8(pe, n, u, g, ru, peeled and i == -1, peeled and i == 0)
                if out:
                    for k in st_of(s):
                        c, g = k // 4, k % 4
                        wait(pe, "exp8", go, k - 2)
                        pe.matmul(PS[0:TC[c], 4 + k % 3, 0:GQ], Kcat[po][:, g, TO[c]:TO[c] + TC[c]],
                                  Qbd[po][:, g, :], start=True, stop=True).then_inc(sem("st8"), 1)
                        if g == 3 and c:
                            pe_pv8(pe, go, po, c - 1)
                    if s == ST_STEPS + 1:
                        pe_pv8(pe, go, po, NT - 1)
                    if s == RECIP - 1:
                        wait(pe, "pv_copied8", go, 1)
                        if mxs:
                            wait(pe, "nm_split8", gm, 1)
                        else:
                            wait(pe, "on8", go, 0)
                        for e in range(4):
                            last = pe.matmul(PS[0:S, 3, GQ + 4 * e:GQ + 4 * e + 4], osb[:, S * e:S * (e + 1)], sumrow,
                                             start=True, stop=True)
                        last.then_inc(sem("sums8"), 1)
                    if s == RECIP + 1:
                        wait(pe, "rec8", go, 1)
                        for e in range(4):
                            for j in range(4):
                                last = pe.matmul(PS[32 * j:32 * j + 32, 3, S * e:S * (e + 1)],
                                                 rec[:, e, j:j + 1].broadcast_to([S, 32]), ident[0:S, 0:S],
                                                 start=True, stop=True, skip_group_check=True)
                        last.then_inc(sem("bcast8"), 1)

        def pe_pv8(pe, go, po, c):
            wait(pe, "exp8", go, 4 * c + 4)
            if c == 0:
                wait(pe, "pv_copied8", go, 0)
            for pr in range(8):
                j, s = pr % 4, pr // 4
                last = pe.matmul(PS[32 * j:32 * j + 32, 7, 2 * S * s:2 * S * (s + 1)],
                                 Vaug[po][0:TC[c], VW * c + 17 * pr:VW * c + 17 * pr + 32],
                                 PT[0:TC[c], c % 2, 2 * S * pr:2 * S * (pr + 1)],
                                 start=(c == 0 and s == 0), stop=(c == NT - 1), skip_group_check=True)
            last.then_inc(sem("pv8"), 1)

        def act_iter8(act, n, i, r, prep, mxs, out):
            gp, go = 2 + B * n + i, B * n + i
            pp = (r + 1) % 3
            for s in range(UNITS):
                if prep and s - 1 in KP and not (isinstance(i, int) and i == -1):
                    act_key(act, gp, KP.index(s - 1), 3)
                if prep and s - 1 in VP and not (isinstance(i, int) and i == -1):
                    k = VP.index(s - 1)
                    if k == 0 and (not isinstance(i, int) or i >= 1):
                        wait(act, "pv8", gp - 3, NT)
                    act_value(act, gp, pp, k, 3)
                if out:
                    for k in st_of(s):
                        c, g = k // 4, k % 4
                        if g == 0:
                            wait(act, "pv8", go, c - 1)
                        wait(act, "st8", go, k + 1)
                        act.activation(PT[0:TC[c], c % 2, GQ * g:GQ * (g + 1)], PS[0:TC[c], 4 + k % 3, 0:GQ],
                                       ACT.Exp, scale=S8).then_inc(sem("exp8"), 1)
            if out:
                wait(act, "pv8", go, NT)
                wait(act, "on8", go, 0)
                act.activation(osb[:, :], PS[:, 7, 0:GQ], ACT.Copy).then_inc(sem("pv_copied8"), 1)

        def dve_iter8(dve, n, i, r, prep, mxs, out):
            gp, gm, go = 2 + B * n + i, 1 + B * n + i, B * n + i
            pp, pm = (r + 1) % 3, r
            for s in range(UNITS):
                if prep and s - 1 in KP and not (isinstance(i, int) and i == -1):
                    dve_key(dve, gp, KP.index(s - 1), 3)
                if mxs and s == UNITS - HEAD:
                    wait(dve, "max_read8", gm, UNITS)
                    wait(dve, "nmT8", gm, 0)
                    dve.tensor_reduce(nm8[:, :], mx8[:, :, :], AX.X, ALU.max, negate=True).then_inc(sem("nm_ready8"), 1)
                    wait(dve, "nm_ready8", gm, 1)
                    dve.tensor_scalar(nmleft[:, :], left4, nm8[0:64, 12:13], None, ALU.mult).then_inc(sem("nm_ready8"), 1)
                if mxs and s == TURN + 1:
                    wait(dve, "nmT8", gm, 1)
                    wait(dve, "mrow_loaded8", gm, 0)
                    dve.tensor_copy(nmTh8[:, :], PS[0:4, 3, 0:GQ]).then_inc(sem("nm_high8"), 1)
                    wait(dve, "nm_high8", gm, 1)
                    dve.tensor_tensor(nmTl8[:, :], PS[0:4, 3, 0:GQ], nmTh8[:, :].bitcast(F32), ALU.subtract)\
                       .then_inc(sem("nm_split8"), 1)
                if out and s == RECIP:
                    wait(dve, "sums8", go, 1)
                    dve.reciprocal(rec[:, :, :], PS[0:S, 3, GQ:GQ + 16].rearrange("p (e j) -> p e j", j=4))\
                       .then_inc(sem("rec8"), 1)
                if isinstance(i, int) and i == -1 and s == UNITS - HEAD:
                    dve.memset(Kcat[0][96:128, :, :].bitcast(F32), 1.0).then_inc(sem("ones_k"), 1)
                    dve.memset(mx8[:, :, :], NEG).then_inc(sem("ones_k"), 1)
                for u, g, _ in units(s, gm, gp, pm, pp, prep, mxs):
                    rows = tile_rows(u // 3)
                    wait(dve, "smax8", g, u + 1)
                    dve.tensor_reduce(mx8[0:rows, u // 3, u % 3:u % 3 + 1], PS[0:rows, u % 3, 0:MC[u % 3]], AX.X,
                                      ALU.max).then_inc(sem("max_read8"), 1)
            if out:
                wait(dve, "bcast8", go, 1)
                dve.tensor_tensor(O8[:, :, cols(i - 1)], osb[:, :].rearrange("p (c q) -> p c q", q=S),
                                  PS[:, 3, 0:GQ].rearrange("p (c q) -> p c q", q=S), ALU.mult).then_inc(sem("on8"), 1)

        def pool_iter8(pool, n, i, r, prep, mxs, out):
            gp = 2 + B * n + i
            pp = (r + 1) % 3
            if prep:
                if not isinstance(i, int) or i >= 1:
                    wait(pool, "st8", gp - 3, 4 * NT)
                    settle(pool)
                pool.tensor_tensor(Qleft[pp][:, :].rearrange("p (g e) -> p g e", e=80)[:, :, 0:16],
                                   QR[:, :, bass.ds((i + 1) * S + 84, 16)].bitcast(F32),
                                   mask4[:, 3:4].unsqueeze(2).broadcast_to([128, 4, 16]), ALU.mult)\
                    .then_inc(sem("qbd_built"), 1)
                for g in range(4):
                    pool.tensor_tensor(Qbd[pp][:, g, :].rearrange("p (j q) -> p j q", j=4),
                                       QR[:, g, cols(i + 1)].bitcast(F32).unsqueeze(1).broadcast_to([128, 4, S]),
                                       mask4.unsqueeze(2).broadcast_to([128, 4, S]), ALU.mult)\
                        .then_inc(sem("qbd_built"), 1)
                if n == 2:
                    if isinstance(i, int) and i == -1:
                        pool.wait_ge(sem("ones_k"), 2 * (n + 1))
                    else:
                        pool.wait_ge(sem("mask_loaded"), 16 * (i + 1))
                        settle(pool)
                    pool.dma_start(Kcat[pp][98:99, :, :], cmask_d[bass.ds(i + 1, 1), :, :].bitcast(U8))\
                        .then_inc(sem("mask_loaded"), 16)
            if isinstance(i, int) and i == -1:
                wait(pool, "qbd_built", gp, 5)
                for q in (1, 2):
                    if q == 2:
                        pool.wait_ge(sem("ones_k2"), 2 * n + 1)
                    pool.memset(Kcat[q][96:128, :, :].bitcast(F32), 1.0).then_inc(sem("ones_k2"), 1)
                pool.wait_ge(sem("ones_k2"), 2 * (n + 1))

        def sp_iter8(sp, n, i, r, prep, mxs, out):
            gp, gm = 2 + B * n + i, 1 + B * n + i
            pp, pm = (r + 1) % 3, r
            if prep:
                wait(sp, "vproj", gp, 0)
                settle(sp)
                sp.dma_start(ctxT8[:, :], ctxT_d[bass.ds(i + 1, 1), :, :].rearrange("a p t -> (a p) t"))\
                    .then_inc(sem("ctx_loaded8"), 16)
                if not isinstance(i, int) or i >= 1:
                    wait(sp, "st8", gp - 3, 4 * NT)
                    settle(sp)
                for part, src in enumerate((kh, kh, kl)):
                    wait(sp, "kl_done" if src is kl else "kh_done", gp, 4)
                    settle(sp)
                    for g in range(4):
                        sp.dma_start(Kcat[pp][32 * part:32 * part + 32, g, :].bitcast(F32), src[32 * g:32 * g + 32, :].bitcast(F32))\
                            .then_inc(sem("kcat_loaded"), 16)
            if mxs:
                wait(sp, "nm_split8", gm, 1)
                settle(sp)
                for row, src in ((96, nmTh8), (97, nmTl8)):
                    sp.dma_start(Qbd[pm][row:row + 1, :, :].bitcast(F32), src[:, :].bitcast(F32)).then_inc(sem("mrow_loaded8"), 16)

        def pipeline(eng, step, n):
            step(eng, n, -1, 2, True, False, False)
            step(eng, n, 0, 0, True, True, False)
            with eng.Fori(0, 2) as t:
                for u in range(3):
                    step(eng, n, 1 + 3 * t + u, (1 + u) % 3, True, True, True)
            step(eng, n, 7, 7 % 3, False, True, True)
            step(eng, n, 8, 8 % 3, False, False, True)

        def banks(lo, hi, rows=S):
            return PS[0:rows, lo:hi, 0:GQ].rearrange("p m (h k) -> p m h k", k=S)

        def by_bank(ap):
            return ap.rearrange("p (m h) k -> p m h k", m=4)

        def self_out(eng, n, g, k):
            wait(eng, "self_out8", g - B, k) if n else wait(eng, "self_out64", g, k)

        def pe_scores(pe, n, g, b, p, st):
            wait(pe, "xq_copied", g, 1)
            if n:
                wait(pe, "qs_copied", g - B, 1)
                wait(pe, "kbd_built", g - B, 1)
            for m in range(4):
                wait(pe, "self_masked", g - 2 * B, m - 3) if n == 2 else wait(pe, "self_exp", g, m - 3)
                if m < 2:
                    wait(pe, "self_v", g, 0)
                    half = slice(64 * m, 64 * m + 64)
                    pe.matmul(PS[0:S, m, GQ:GQ + 64], st["xq"][:, p, :], (wcol(n, "sv", 0) if n else ident)[:, half],
                              start=True, stop=True)
                keys = st["Kbd"][:, p, 4 * m:4 * m + 4, :] if n else BIG[:, 4 * m:4 * m + 4, cols(b)]
                pe.matmul(PS[0:S, m, 0:GQ], (st["qs"] if n else st["xq"])[:, p, :], keys, start=True, stop=True)\
                    .then_inc(sem("self_scores"), 1)

        def pe_turn(pe, n, g, st):
            wait(pe, "self_norm", g, 1)
            self_out(pe, n, g, 0)
            for h in range(H):
                last = pe.transpose(PS[0:S, 4 + h // 4, S * (h % 4):S * (h % 4 + 1)], st["Pn"][:, h, :], ident[0:S, 0:S])
            last.then_inc(sem("self_turned"), 1)

        def pe_self_pv(pe, n, g, p, st):
            wait(pe, "self_pt", g, 1)
            wait(pe, "self_v", g, 1)
            if n:
                for pr in range(8):
                    j, s = pr % 4, pr // 4
                    last = pe.matmul(PS[32 * j:32 * j + 32, 4, 2 * S * s:2 * S * (s + 1)],
                                     st["Vn"][:, p, 16 * pr:16 * pr + 32], PT[0:S, p, 2 * S * pr:2 * S * (pr + 1)],
                                     start=(s == 0), stop=True, skip_group_check=True)
            else:
                for m in range(4):
                    last = pe.matmul(PS[:, 4 + m, 0:GQ], st["Vn"][:, p, 0:128], PT[0:S, p, GQ * m:GQ * (m + 1)],
                                     start=True, stop=True)
            last.then_inc(sem("self_pv"), 1)

        def dve_max(dve, n, g, b, st):
            for m in range(4):
                heads = slice(4 * m, 4 * m + 4)
                wait(dve, "self_scores", g, m + 1)
                wait(dve, "self_exp", g, m - 3)
                src = PS[0:S, m, 0:GQ].rearrange("p (h k) -> p h k", k=S)
                if n == 2:
                    dve.tensor_tensor(st["Ps"][:, heads, :], src, cmb[:, bass.ds(b, 1), :].broadcast_to([S, 4, S]), ALU.add)\
                       .then_inc(sem("self_masked"), 1)
                    wait(dve, "self_masked", g - 2 * B, m + 1)
                    src = st["Ps"][:, heads, :]
                dve.tensor_reduce(st["smx"][:, heads], src, AX.X, ALU.max, negate=True).then_inc(sem("self_max"), 1)

        def dve_values(dve, n, g, p, st):
            wait(dve, "self_exp", g, 2)
            wait(dve, "self_pv", g, -1)
            v = PS[0:S, 0:2, GQ:GQ + 64]
            dst = st["Vn"][:, p, 0:128].rearrange("p (a e) -> p a e", a=2)
            if n:
                bv = W[0:S, WOFF[n]["bv"]:WOFF[n]["bv"] + 128].rearrange("p (a e) -> p a e", a=2)
                dve.tensor_tensor(dst, v, bv, ALU.add).then_inc(sem("self_v"), 1)
            else:
                dve.tensor_copy(dst, v).then_inc(sem("self_v"), 1)

        def dve_rec(dve, n, g, st):
            wait(dve, "self_exp", g, 4)
            wait(dve, "self_norm", g, 0)
            dve.reciprocal(st["srec"][:, :], st["ssum"][:, :]).then_inc(sem("self_rec"), 1)

        def dve_out(dve, n, g, b):
            wait(dve, "self_pv", g, 1)
            if not n:
                dve.tensor_copy(BIG[:, :, cols(b)].rearrange("p (m h) q -> p m h q", m=4), banks(4, 8, 128))\
                   .then_inc(sem("self_out64"), 1)
                return
            dve.tensor_copy(O8[:, :, cols(b)], PS[:, 4, 0:GQ].rearrange("p (c q) -> p c q", q=S))\
               .then_inc(sem("self_out8"), 1)

        def act_exp(act, n, g, p, st):
            wait(act, "self_norm", g, -1)
            wait(act, "self_rec", g, 0)
            for m in range(4):
                wait(act, "self_max", g, m + 1)
                for h in range(4 * m, 4 * m + 4):
                    src = st["Ps"][:, h, :] if n == 2 else PS[0:S, m, S * (h % 4):S * (h % 4) + S]
                    last = act.activation(st["Pe"][:, p, h, :], src, ACT.Exp, bias=st["smx"][:, h:h + 1],
                                          accum_out=st["ssum"][:, h:h + 1])
                last.then_inc(sem("self_exp"), 1)

        def act_turned(act, n, g, p):
            wait(act, "self_turned", g, 1)
            wait(act, "self_pv", g, -1)
            act.activation(PT[0:S, p, :].rearrange("p (m k) -> p m k", m=4), PS[0:S, 4:8, 0:GQ], ACT.Copy)\
               .then_inc(sem("self_pt"), 1)

        def pool_front(pool, n, g, b, p, st):
            wait(pool, "self_scores", g, -4)
            settle(pool)
            pool.tensor_copy(st["xq"][:, p, :], (x[:, cols(b)] if n == 1 else YS[:, 0, cols(b)])).then_inc(sem("xq_copied"), 1)
            if n:
                pool.tensor_copy(st["qs"][:, p, :], qT[:, cols(b)]).then_inc(sem("qs_copied"), 1)
                pool.tensor_tensor(st["Kbd"][:, p, :, :], kT[:, cols(b)].unsqueeze(1).broadcast_to([128, H, S]),
                                   mask16.unsqueeze(2).broadcast_to([128, H, S]), ALU.mult)\
                    .then_inc(sem("kbd_built"), 1)

        def pool_norm(pool, n, g, p, st):
            wait(pool, "self_rec", g, 1)
            wait(pool, "self_turned", g, 0)
            settle(pool)
            pool.tensor_tensor(st["Pn"][:, :, :], st["Pe"][:, p, :, :], st["srec"][:, :].unsqueeze(2).broadcast_to([S, H, S]),
                               ALU.mult).then_inc(sem("self_norm"), 1)

        def self_step(eng, who, n, st, b, p, before, after):
            g = 1 + B * n + b
            if who == "pe":
                if after:
                    pe_scores(eng, n, g + 1, b + 1, 1 - p, st)
                if before:
                    pe_self_pv(eng, n, g - 1, 1 - p, st)
                pe_turn(eng, n, g, st)
            elif who == "dve":
                dve_rec(eng, n, g, st)
                if after:
                    dve_max(eng, n, g + 1, b + 1, st)
                if before:
                    dve_out(eng, n, g - 1, b - 1)
                if after:
                    dve_values(eng, n, g + 1, 1 - p, st)
            elif who == "act":
                if after:
                    act_exp(eng, n, g + 1, 1 - p, st)
                act_turned(eng, n, g, p)

        def self_attention(eng, who, n, st):
            g0, gl = 1 + B * n, B * (n + 1)
            if who == "pool":
                pool_front(eng, n, g0, 0, 0, st)
                pool_front(eng, n, g0 + 1, 1, 1, st)
                with eng.Fori(0, B // 2 - 1) as t:
                    for p in range(2):
                        b = 2 * t + p
                        pool_norm(eng, n, g0 + b, p, st)
                        pool_front(eng, n, g0 + b + 2, b + 2, p, st)
                for p in range(2):
                    pool_norm(eng, n, gl - 1 + p, p, st)
                return
            if who == "pe":
                pe_scores(eng, n, g0, 0, 0, st)
            elif who == "dve":
                dve_max(eng, n, g0, 0, st)
                dve_values(eng, n, g0, 0, st)
            else:
                act_exp(eng, n, g0, 0, st)
            self_step(eng, who, n, st, 0, 0, False, True)
            with eng.Fori(0, B // 2 - 1) as t:
                for u in range(2):
                    self_step(eng, who, n, st, 1 + 2 * t + u, 1 - u, True, True)
            self_step(eng, who, n, st, B - 1, 1, True, False)
            if who == "pe":
                pe_self_pv(eng, n, gl, 1, st)
            elif who == "dve":
                dve_out(eng, n, gl, B - 1)

        EXP, TURN1 = 3, 14
        SUM, OB, BC, ON = TURN1 + 1, TURN1 + 2, TURN1 + 3, TURN1 + 4
        STEPS1 = 4 * NT

        def late(s, lag, p, cur, prev):
            k = s - lag
            u = k % STEPS1
            if (cur and 0 <= k) or (prev and k < 0):
                return [(k, u, u // NT, p if k >= 0 else 1 - p)]
            return []

        def group_done(s, lag, p, cur, prev):
            return [((k - NT + 1) // NT, g) for k, u, g, _ in late(s, lag, p, cur, prev) if u % NT == NT - 1]

        def steps1(cur):
            return range(STEPS1 if cur else ON)

        def part1(k):
            return slice(482 * k, 482 * k + MC[k])

        def pe_iter1(pe, b, p, cur, prev, more):
            gb = b + 1
            for s in steps1(cur):
                for k, u, g, _ in late(s, TURN1, p, cur, prev):
                    c = u % NT
                    third = (TO[c] + TC[c] - 1) // 482
                    wait(pe, "exp1", gb, k - c + 9 + third + 1)
                    wait(pe, "low1", gb, k - 1)
                    for j in range(4):
                        last = pe.transpose(PS[0:TC[c], 4 + u % 2, S * j:S * (j + 1)],
                                            P1[:, g % 2, j, TO[c]:TO[c] + TC[c]], ident[0:S, 0:S])
                    last.then_inc(sem("turned1"), 1)
                if cur:
                    g, h = s // 12, s // 3
                    if s == 0:
                        wait(pe, "ctx_split", gb, 2)
                    if s % 12 == 0:
                        wait(pe, "q_split", gb, 2 * g + 2)
                    wait(pe, "exp1", gb, s - 3)
                    q = slice(S * (h % 4), S * (h % 4) + S)
                    for a, (ql, cc) in enumerate(((Qh, ch), (Ql, ch), (Qh, cl))):
                        last = pe.matmul(PS[0:S, s % 4, 0:MC[s % 3]], ql[:, g % 2, q], cc[p][:, part1(s % 3)],
                                         start=(a == 0), stop=(a == 2))
                    last.then_inc(sem("scored1"), 1)
                for k, u, g, r in late(s, SUM, p, cur, prev):
                    c = u % NT
                    if c == 0:
                        wait(pe, "on1", gb, k // NT - 1)
                        if g == 0:
                            wait(pe, "cn_split", gb, 2)
                    wait(pe, "low1", gb, k + 1)
                    for a, (n, x_) in enumerate(((nh, Ph), (nl, Ph), (nh, Pl))):
                        last = pe.matmul(PS[0:C, 6 + g % 2, 0:GQ], n[r][0:TC[c], c, :], x_[0:TC[c], u % 2, :],
                                         start=(c == 0 and a == 0), stop=(c == NT - 1 and a == 2))
                    last.then_inc(sem("pv1"), 1)
                for kg, g in group_done(s, BC, p, cur, prev):
                    wait(pe, "rec1", gb, kg + 1)
                    wait(pe, "pv_copied1", gb, kg + 1)
                    for j in range(4):
                        last = pe.matmul(PS[0:C, 6 + g % 2, S * j:S * (j + 1)], inv1[:, j:j + 1].broadcast_to([S, C]),
                                         ident[0:S, 0:S], start=True, stop=True)
                    last.then_inc(sem("bcast1"), 1)

        def act_iter1(act, b, p, cur, prev, more):
            gb = b + 1
            for s in steps1(cur):
                for k, u, g, _ in late(s, EXP, p, cur, prev):
                    h = u // 3
                    wait(act, "shift1", gb, (k - u % 3) // 3 + 1)
                    if u % 12 == 0:
                        wait(act, "turned1", gb, k - 12)
                        wait(act, "rec1", gb, k // 12 - 3)
                    act.activation(P1[:, g % 2, h % 4, part1(u % 3)], PS[0:S, u % 4, 0:MC[u % 3]], ACT.Exp,
                                   bias=shift1[:, h:h + 1], accum_out=sums1[:, h, u % 3:u % 3 + 1])\
                       .then_inc(sem("exp1"), 1)
                for k, u, g, _ in late(s, TURN1, p, cur, prev):
                    c = u % NT
                    wait(act, "turned1", gb, k + 1)
                    wait(act, "pv1", gb, k - 1)
                    act.activation(Ph[0:TC[c], u % 2, :], PS[0:TC[c], 4 + u % 2, 0:GQ], ACT.Copy)\
                       .then_inc(sem("high1"), 1)
                for kg, g in group_done(s, OB, p, cur, prev):
                    wait(act, "pv1", gb, NT * (kg + 1))
                    wait(act, "on1", gb, kg)
                    act.activation(ob1[:, :], PS[0:C, 6 + g % 2, 0:GQ], ACT.Copy).then_inc(sem("pv_copied1"), 1)

        def dve_iter1(dve, b, p, cur, prev, more):
            gb = b + 1
            for s in steps1(cur):
                if cur:
                    wait(dve, "scored1", gb, s + 1)
                    dve.tensor_reduce(mx1[:, s // 3, s % 3:s % 3 + 1], PS[0:S, s % 4, 0:MC[s % 3]], AX.X, ALU.max)\
                       .then_inc(sem("max_read1"), 1)
                if cur and s % 3 == 2:
                    h = s // 3
                    wait(dve, "max_read1", gb, s + 1)
                    dve.tensor_reduce(shift1[:, h:h + 1], mx1[:, h, :], AX.X, ALU.max, negate=True)\
                       .then_inc(sem("shift1"), 1)
                for k, u, g, _ in late(s, TURN1, p, cur, prev):
                    c = u % NT
                    wait(dve, "high1", gb, k + 1)
                    dve.tensor_tensor(Pl[0:TC[c], u % 2, :], PS[0:TC[c], 4 + u % 2, 0:GQ],
                                      Ph[0:TC[c], u % 2, :].bitcast(F32), ALU.subtract).then_inc(sem("low1"), 1)
                for kg, g in group_done(s, OB, p, cur, prev):
                    wait(dve, "exp1", gb, 12 * (kg + 1))
                    dve.tensor_reduce(sum1[:, :], sums1[:, 4 * g:4 * g + 4, :], AX.X, ALU.add).then_inc(sem("sum1"), 1)
                    wait(dve, "sum1", gb, kg + 1)
                    wait(dve, "bcast1", gb, kg)
                    dve.reciprocal(inv1[:, :], sum1[:, :]).then_inc(sem("rec1"), 1)
                for kg, g in group_done(s, ON, p, cur, prev):
                    wait(dve, "bcast1", gb, kg + 1)
                    dve.tensor_tensor(BIG[0:C, 4 * g:4 * g + 4, cols(b if kg >= 0 else b - 1)],
                                      ob1[:, :].rearrange("p (h q) -> p h q", q=S),
                                      PS[0:C, 6 + g % 2, 0:GQ].rearrange("p (h q) -> p h q", q=S), ALU.mult)\
                       .then_inc(sem("on1"), 1)

        def pool_queries(pool, gb, b, g):
            wait(pool, "scored1", gb, 12 * (g - 1))
            settle(pool)
            q = BIG[0:C, 4 * g:4 * g + 4, cols(b)]
            high = Qh[:, g % 2, :].rearrange("p (h q) -> p h q", q=S)
            low = Ql[:, g % 2, :].rearrange("p (h q) -> p h q", q=S)
            pool.tensor_copy(high, q).then_inc(sem("q_split"), 1)
            wait(pool, "q_split", gb, 2 * g + 1)
            settle(pool)
            pool.tensor_tensor(low, q, high.bitcast(F32), ALU.subtract).then_inc(sem("q_split"), 1)

        def raw_ctx():
            return raw1[0:C, :]

        def raw_cn():
            return raw1[:, 0:NT * C].rearrange("p (c e) -> p c e", e=C)

        def pool_context(pool, gb, loaded, name, raw, high, low):
            wait(pool, loaded, gb, 16)
            settle(pool)
            pool.tensor_copy(high, raw).then_inc(sem(name), 1)
            wait(pool, name, gb, 1)
            settle(pool)
            pool.tensor_tensor(low, raw, high.bitcast(F32), ALU.subtract).then_inc(sem(name), 1)

        def pool_iter1(pool, b, p, cur, prev, more):
            gb = b + 1
            if not cur:
                return
            pool_queries(pool, gb, b, 1)
            if more:
                wait(pool, "scored1", gb, 0)
                settle(pool)
                pool_context(pool, gb + 1, "ctx_loaded1", "ctx_split", raw_ctx(), ch[1 - p][:, :], cl[1 - p][:, :])
            pool_queries(pool, gb, b, 2)
            if more:
                wait(pool, "pv1", gb, 0)
                settle(pool)
                pool_context(pool, gb + 1, "cn_loaded", "cn_split", raw_cn(), nh[1 - p][:, :, :], nl[1 - p][:, :, :])
            pool_queries(pool, gb, b, 3)
            if more:
                pool_queries(pool, gb + 1, b + 1, 0)

        def sp_load1(sp, b):
            wait(sp, "cn_split", b + 1, 0)
            settle(sp)
            sp.dma_start(raw_ctx(), ctxT_d[bass.ds(b, 1), 0:C, :].rearrange("a p t -> (a p) t"))\
                .then_inc(sem("ctx_loaded1"), 16)
            wait(sp, "ctx_split", b + 1, 2)
            settle(sp)
            sp.dma_start(raw_cn(), ctxN_d[bass.ds(b, 1), :, :, :].rearrange("a p c e -> (a p) c e"))\
                .then_inc(sem("cn_loaded"), 16)

        def sp_iter1(sp, b, p, cur, prev, more):
            if more:
                sp_load1(sp, b + 1)

        def pipeline1(eng, step):
            if eng is nc.sync:
                sp_load1(eng, 0)
            if eng is nc.gpsimd:
                pool_context(eng, 1, "ctx_loaded1", "ctx_split", raw_ctx(), ch[0][:, :], cl[0][:, :])
                pool_context(eng, 1, "cn_loaded", "cn_split", raw_cn(), nh[0][:, :, :], nl[0][:, :, :])
                big_ready(eng, 2)
                pool_queries(eng, 1, 0, 0)
            step(eng, 0, 0, True, False, True)
            with eng.Fori(0, B // 2 - 1) as t:
                for u in range(2):
                    step(eng, 1 + 2 * t + u, 1 - u, True, True, True)
            step(eng, B - 1, 1, True, True, False)
            step(eng, B, 0, False, True, False)

        def fuse_pe(pe, kind, a, b, rows, width):
            for t in range(2):
                tile_free(pe, f"fuse{kind}{t}")
                k = TI[f"fuse{kind}{t}"] % 2
                for i in range(4):
                    for m in range(2):
                        h = slice(64 * m, 64 * m + 64)
                        last = pe.matmul(PS[0:rows, 2 * k + m, 128 * i:128 * i + width], WF[h, a, 4 * t + i, 0:rows],
                                         WF[h, b, 4 * t + i, 0:width], start=True, stop=True)
                last.then_inc(sem("tile_full"), 1)

        def fuse_act(act, kind, dst, rows, width, scale=1.0):
            for t in range(2):
                name = f"fuse{kind}{t}"
                tile_full(act, name)
                k = TI[name] % 2
                src = PS[0:rows, 2 * k:2 * k + 2, :].rearrange("p m (i e) -> p m i e", e=128)[:, :, :, 0:width]
                out = dst[0:rows, 8 * t:8 * t + 8, 0:width].rearrange("p (i m) e -> p m i e", m=2)
                taken(act.activation(out, src, ACT.Copy, scale=scale), name)

        FUSE = [("A", 0, 1, 128, 128, WA1), ("B", 2, 3, 128, 128, WB1), ("C", 4, 5, 128, C, WA2), ("D", 6, 7, C, 128, WB2)]

        def big_copy(eng, who, kind, rows):
            for h in range(0 if who == "act" else 1, H, 2):
                name = f"{kind}64_{h}"
                tile_full(eng, name)
                dst = halves(BIG[0:rows, h, :])
                if who == "act":
                    ins = eng.activation(dst, tile(name, rows=rows), ACT.Copy)
                else:
                    ins = eng.tensor_copy(dst, tile(name, rows=rows))
                taken(ins, name)

        def big_ready(eng, times):
            kind = "k" if times == 1 else "q"
            gone(eng, f"{kind}64_{H - 2}", f"{kind}64_{H - 1}")

        def out_terms(n):
            return [(wcol(n, "co", i), O8[:, i, :]) for i in range(4)]

        block = ctx.enter_context(nc.Block())

        @block.sync
        def _(sp):
            credit(sp, "sync")
            sp.dma_start(W[:, 0:W0["end"]], w0_d[:, :]).then_inc(sem("w0_in"), 16)
            sp.dma_start(x[:, :], xT_d[:, :]).then_inc(sem("x_in"), 16)
            sp.dma_start(bias[:, :], bias_d[:, :]).then_inc(sem("bias_in"), 16)
            sp.dma_start(const[:, :], const_d[:, :]).then_inc(sem("const_in"), 16)
            pipeline(sp, sp_iter8, 0)
            x_ready(sp, 1)
            sp.dma_start(WF[:, :, :, :], wf_d[:, :, :, :]).then_inc(sem("wf_in"), 16)
            sp.dma_start(FF1[:, :], ff1_d[:, :]).then_inc(sem("ff1_in"), 16)
            sp.dma_start(FF2[:, :], ff2_d[:, :]).then_inc(sem("ff2_in"), 16)
            x_ready(sp, 2)
            pipeline1(sp, sp_iter1)
            x_ready(sp, 3)
            sp.dma_start(W[:, :], w2_d[:, :]).then_inc(sem("w2_in"), 16)
            x_ready(sp, 5)
            pipeline(sp, sp_iter8, 1)
            x_ready(sp, 9)
            sp.dma_start(W[:, 0:W3["end"]], w3_d[:, :]).then_inc(sem("w3_in"), 16)
            sp.dma_start(tmask[:, :, :], tmask_d[:, :, :].bitcast(U8)).then_inc(sem("tmask_in"), 16)
            x_ready(sp, 11)
            pipeline(sp, sp_iter8, 2)
            x_ready(sp, 13)
            sp.dma_start(out_d[:, :], x[:, :]).then_inc(sem("out_stored"), 16)
            sp.wait_ge(sem("out_stored"), 16)

        @block.tensor
        def _(pe):
            credit(pe, "tensor")
            for name in ("w0_in", "x_in", "const_in"):
                pe.wait_ge(sem(name), 16)
            for j in range(3):
                prep0(pe, 0, j)
            qr_pe(pe, 0, x)
            pe.wait_ge(sem("tile_taken0"), (TI["qr0_2"] // 2) + 1)
            pe.wait_ge(sem("tile_taken1"), (TI["qr0_3"] // 2) + 1)
            pipeline(pe, pe_iter8, 0)
            wait(pe, "on8", B, 1)
            dense(pe, "proj0", out_terms(0))
            ln_pe(pe, 0, x)
            pe.wait_ge(sem("wf_in"), 16)
            for kind, a, b, rows, width, _ in FUSE:
                fuse_pe(pe, kind, a, b, rows, width)
            pe.wait_ge(sem("y_ready"), 1)
            for h in range(H):
                dense(pe, f"k64_{h}", [(WA1[:, h, :], y)])
            big_ready(pe, 1)
            self_attention(pe, "pe", 0, self1b)
            wait(pe, "self_out64", B, 1)
            dense(pe, "proj1", [(WB1[:, h, :], BIG[:, h, :]) for h in range(H)])
            ln_pe(pe, 1, x)
            pe.wait_ge(sem("y_ready"), 2)
            for h in range(H):
                dense(pe, f"q64_{h}", [(WA2[:, h, 0:C], y)], rows=C)
            pipeline1(pe, pe_iter1)
            wait(pe, "on1", B, 4)
            dense(pe, "proj2", [(WB2[0:C, h, :], BIG[0:C, h, :]) for h in range(H)])
            ln_pe(pe, 2, x)
            pe.wait_ge(sem("y_ready"), 3)
            pe.wait_ge(sem("ff1_in"), 16)
            pe.wait_ge(sem("ff2_in"), 16)
            for t in range(4):
                dense(pe, f"gate{t}", [(FF1[:, 512 + 128 * t:640 + 128 * t], y)])
                dense(pe, f"lin{t}", [(FF1[:, 128 * t:128 * t + 128], y)])
            gone(pe, "lin2", "lin3")
            dense(pe, "ff2", [(FF2[:, 128 * t:128 * t + 128], U[:, t, :]) for t in range(4)])
            pe.wait_ge(sem("w2_in"), 16)
            x_ready(pe, 4)
            dense(pe, "sq1", [(wcol(1, "sq", 0), x)])
            dense(pe, "sk1", [(wcol(1, "sk", 0), x)])
            gone(pe, "sq1", "sk1")
            self_attention(pe, "pe", 1, self8b)
            wait(pe, "self_out8", B, 1)
            dense(pe, "proj3", [(wcol(1, "so", i), O8[:, i, :]) for i in range(4)])
            ln_pe(pe, 3, x, 1)
            x_ready(pe, 6)
            qr_pe(pe, 1, x)
            pe.wait_ge(sem("qr_split"), 8)
            pipeline(pe, pe_iter8, 1)
            wait(pe, "on8", 2 * B, 1)
            dense(pe, "proj4", out_terms(1))
            ln_pe(pe, 4, x)
            x_ready(pe, 8)
            for t in range(4):
                dense(pe, f"h1_{t}", [(wcol(1, "w1", t), x)])
            gone(pe, "h1_2", "h1_3")
            for t in range(4):
                dense(pe, f"h2_{t}", [(wcol(1, "w2", 4 * k + t), U[:, k, :]) for k in range(4)])
            gone(pe, "h2_2", "h2_3")
            dense(pe, "h3", [(wcol(1, "w3", k), U2[:, k, :]) for k in range(4)])
            ln_pe(pe, 5, x)
            ln_pe(pe, 6, x)
            pe.wait_ge(sem("w3_in"), 16)
            pe.wait_ge(sem("y_ready"), 4)
            dense(pe, "sq2", [(wcol(2, "sq", 0), y)])
            dense(pe, "sk2", [(wcol(2, "sk", 0), y)])
            gone(pe, "sq2", "sk2")
            self_attention(pe, "pe", 2, self8b)
            wait(pe, "self_out8", 2 * B, 1)
            dense(pe, "proj5", [(wcol(2, "so", i), O8[:, i, :]) for i in range(4)])
            ln_pe(pe, 7, x, 2)
            pe.wait_ge(sem("y_ready"), 5)
            qr_pe(pe, 2, y)
            pe.wait_ge(sem("qr_split"), 12)
            pipeline(pe, pe_iter8, 2)
            wait(pe, "on8", 3 * B, 1)
            dense(pe, "proj6", out_terms(2))
            ln_pe(pe, 8, x)
            pe.wait_ge(sem("y_ready"), 6)
            for t in range(4):
                dense(pe, f"g1_{t}", [(wcol(2, "w1", t), y)])
            gone(pe, "g1_2", "g1_3")
            dense(pe, "g2", [(wcol(2, "w3", k), U[:, k, :]) for k in range(4)])

        @block.scalar
        def _(act):
            credit(act, "scalar")
            act.wait_ge(sem("bias_in"), 16)
            for j in range(3):
                prep0(act, 0, j)
            qr_act(act, 0)
            pipeline(act, act_iter8, 0)
            ln_act(act, 0)
            for kind, _, _, rows, width, dst in FUSE:
                fuse_act(act, kind, dst, rows, width, S64 if kind in "AC" else 1.0)
            big_copy(act, "act", "k", 128)
            self_attention(act, "act", 0, self1b)
            ln_act(act, 1)
            big_copy(act, "act", "q", C)
            pipeline1(act, act_iter1)
            ln_act(act, 2)
            for t in range(4):
                if t >= 2:
                    gone(act, f"lin{t - 2}")
                tile_full(act, f"gate{t}")
                taken(act.activation(halves((xc, sq)[t % 2]), tile(f"gate{t}"), ACT.Gelu_apprx_tanh,
                                     bias=bcol(f"bf1_{4 + t}")), f"gate{t}")
            for name, b, dst in (("sq1", "b2q", qT), ("sk1", "b2k", kT)):
                tile_full(act, name)
                taken(act.activation(halves(dst[:, :]), tile(name), ACT.Identity, bias=bcol(b)), name)
            self_attention(act, "act", 1, self8b)
            ln_act(act, 3, 1)
            qr_act(act, 1)
            pipeline(act, act_iter8, 1)
            ln_act(act, 4)
            ln_act(act, 5)
            ln_act(act, 6)
            for name, b, dst in (("sq2", "b3q", qT), ("sk2", "b3k", kT)):
                tile_full(act, name)
                taken(act.activation(halves(dst[:, :]), tile(name), ACT.Identity, bias=bcol(b)), name)
            self_attention(act, "act", 2, self8b)
            ln_act(act, 7, 2)
            qr_act(act, 2)
            pipeline(act, act_iter8, 2)
            ln_act(act, 8)
            for t in range(4):
                tile_full(act, f"g1_{t}")
                taken(act.activation(halves(U[:, t, :]), tile(f"g1_{t}"), ACT.Gelu, bias=bcol(f"b31_{t}")), f"g1_{t}")


        def relu(dve, kind, b, dst):
            for t in range(4):
                tile_full(dve, f"{kind}_{t}")
                taken(dve.tensor_scalar(halves(dst[:, t, :]), tile(f"{kind}_{t}"), bcol(f"{b}_{t}"), 0.0, ALU.add, ALU.max),
                      f"{kind}_{t}")

        @block.vector
        def _(dve):
            credit(dve, "vector")
            dve.wait_ge(sem("bias_in"), 16)
            dve.wait_ge(sem("x_in"), 16)
            for j in range(3):
                prep0(dve, 0, j)
            qr_dve(dve, 0)
            pipeline(dve, dve_iter8, 0)
            add_to_x(dve, "proj0", "bo0", 0)
            ln_dve(dve, 0, x[:, :], y, "l1g1", "l1b1", "y_ready")
            big_copy(dve, "dve", "k", 128)
            self_attention(dve, "dve", 0, self1b)
            add_to_x(dve, "proj1", "b1o1", 1)
            x_ready(dve, 2)
            ln_dve(dve, 1, x[:, :], y, "l1g2", "l1b2", "y_ready")
            big_copy(dve, "dve", "q", C)
            pipeline1(dve, dve_iter1)
            add_to_x(dve, "proj2", "b1o2", 2)
            x_ready(dve, 3)
            ln_dve(dve, 2, x[:, :], y, "l1g3", "l1b3", "y_ready")
            for t in range(4):
                gone(dve, f"gate{t}")
                tile_full(dve, f"lin{t}")
                taken(dve.scalar_tensor_tensor(halves(U[:, t, :]), tile(f"lin{t}"), bcol(f"bf1_{t}"),
                                               halves((xc, sq)[t % 2]), ALU.add, ALU.mult), f"lin{t}")
            add_to_x(dve, "ff2", "bf2", 3)
            self_attention(dve, "dve", 1, self8b)
            add_to_x(dve, "proj3", "b2so", 4)
            x_ready(dve, 5)
            ln_dve(dve, 3, x[:, :], x[:, :], "l2g", "l2b", "x_normed", 1)
            qr_dve(dve, 1)
            pipeline(dve, dve_iter8, 1)
            add_to_x(dve, "proj4", "b2co", 6)
            x_ready(dve, 7)
            ln_dve(dve, 4, x[:, :], x[:, :], "l2g", "l2b", "x_normed")
            relu(dve, "h1", "b21", U)
            relu(dve, "h2", "b22", U2)
            add_to_x(dve, "h3", "b23", 8)
            x_ready(dve, 9)
            ln_dve(dve, 5, x[:, :], x[:, :], "l2g", "l2b", "x_normed")
            x_ready(dve, 10)
            ln_dve(dve, 6, x[:, :], y, "l3g1", "l3b1", "y_ready")
            dve.wait_ge(sem("tmask_in"), 16)
            dve.scalar_tensor_tensor(cmb[:, :, :], tmask[:, :, :], NEG, causal.unsqueeze(1).broadcast_to([S, B, S]),
                                     ALU.mult, ALU.add).then_inc(sem("cmb_ready"), 1)
            dve.wait_ge(sem("cmb_ready"), 1)
            self_attention(dve, "dve", 2, self8b)
            add_to_x(dve, "proj5", "b3p", 10)
            x_ready(dve, 11)
            ln_dve(dve, 7, x[:, :], y, "l3g2", "l3b2", "y_ready", 2)
            qr_dve(dve, 2)
            pipeline(dve, dve_iter8, 2)
            add_to_x(dve, "proj6", "b3o", 11)
            x_ready(dve, 12)
            ln_dve(dve, 8, x[:, :], y, "l3g3", "l3b3", "y_ready")
            add_to_x(dve, "g2", "b32", 12)

        @block.gpsimd
        def _(pool):
            def ones_v():
                for p in range(3):
                    pool.memset(Vaug[p][:, :], 1.0).then_inc(sem("ones_v"), 1)
                    pool.memset(Qleft[p][:, :].bitcast(F32), 0.0).then_inc(sem("zero_q"), 1)

            credit(pool, "gpsimd")
            ones_v()
            pool.wait_ge(sem("const_in"), 16)
            pool.wait_ge(sem("zero_q"), 3)
            pool.wait_ge(sem("qr_split"), 4)
            pipeline(pool, pool_iter8, 0)
            pool.wait_ge(sem("y_ready"), 1)
            self_attention(pool, "pool", 0, self1b)
            x_ready(pool, 2)
            pipeline1(pool, pool_iter1)
            gone(pool, "sq1", "sk1")
            pool.memset(self8b["Vn"][:, :, 128:144], 0.0).then_inc(sem("vn_pad"), 1)
            self_attention(pool, "pool", 1, self8b)
            x_ready(pool, 5)
            ones_v()
            pool.wait_ge(sem("zero_q"), 6)
            pool.wait_ge(sem("qr_split"), 8)
            pipeline(pool, pool_iter8, 1)
            gone(pool, "sq2", "sk2")
            pool.memset(self8b["Vn"][:, :, 128:144], 0.0).then_inc(sem("vn_pad"), 1)
            self_attention(pool, "pool", 2, self8b)
            x_ready(pool, 11)
            ones_v()
            pool.wait_ge(sem("zero_q"), 9)
            pool.wait_ge(sem("qr_split"), 12)
            pipeline(pool, pool_iter8, 2)


def kernel(**inputs):
    import numpy as np
    import concourse.bacc as bacc
    from concourse.bass_utils import run_bass_kernel_spmd as run

    a = {k: np.asarray(v) for k, v in inputs.items()}
    f = np.float32

    def pad(m, rows=128, width=None):
        m = m if m.ndim == 2 else m.reshape(len(m), -1)
        out = np.zeros((rows, width or m.shape[1]), f)
        out[:m.shape[0], :m.shape[1]] = m
        return out

    def query_part(w):
        out = np.zeros((128, 4, 4, 32), f)
        for part in range(3):
            out[:, :, part, :] = w.reshape(128, 4, 32)
        return out.reshape(128, 512)

    def query_bias(b, masked):
        out = np.zeros((4, 4, 32), f)
        for part in range(3):
            out[:, part, :] = b.reshape(4, 32)
        out[:, 3, 2] = NEG if masked else 0.0
        return out.reshape(4, 128)

    def out_part(w):
        out = np.zeros((2, 2, 4, 32, 128), f)
        wh = w.reshape(2, 4, 2, 8, 128)
        for e in range(2):
            out[:, e, :, 8 * e:8 * e + 8, :] = wh[:, :, e]
        return out.reshape(4, 128, 128).transpose(1, 0, 2).reshape(128, 512)

    def with_row(w, b):
        return pad(np.concatenate([w, b[None]], 0))

    zero = np.zeros(128, f)
    L0 = {k: a["L0_xattn_W" + k].T for k in "qkvo"}
    w0 = np.concatenate([query_part(L0["q"]), with_row(L0["k"], zero), with_row(L0["v"], zero), out_part(L0["o"])], 1)

    p2, p3 = "L2_xattn_", "L3_xattn_"
    qkv2, b2, qkv3, b3 = a[p2 + "w_qkv"], a[p2 + "b_qkv"], a[p3 + "qkv_w"], a[p3 + "qkv_b"]

    def tiles(w):
        return w.reshape(-1, 128, w.shape[1]).transpose(1, 0, 2).reshape(128, -1)

    def rows_of(b):
        return np.broadcast_to(b[None], (128, 128))

    w2 = np.concatenate([query_part(a[p2 + "w_q"]), with_row(a[p2 + "w_k"], a[p2 + "b_k"]),
                         with_row(a[p2 + "w_v"], a[p2 + "b_v"]), out_part(a[p2 + "w_co"]),
                         qkv2[:, 0:128], qkv2[:, 128:256], qkv2[:, 256:384], rows_of(b2[256:384]),
                         out_part(a[p2 + "w_so"]), a[p2 + "w1"], tiles(a[p2 + "w2"]), tiles(a[p2 + "w3"])], 1)
    w3 = np.concatenate([query_part(a[p3 + "q_w"]), with_row(a[p3 + "k_w"], a[p3 + "k_b"]),
                         with_row(a[p3 + "v_w"], a[p3 + "v_b"]), out_part(a[p3 + "out_w"]),
                         qkv3[:, 0:128], qkv3[:, 128:256], qkv3[:, 256:384], rows_of(b3[256:384]),
                         out_part(a[p3 + "proj_w"]), a[p3 + "mlp1_w"], tiles(a[p3 + "mlp2_w"])], 1)

    p1 = "L1_xattn_"

    def by_head(w):
        out = np.zeros((128, 8, 128), f)
        out[:, :, :w.shape[1]] = w.reshape(8, 128, w.shape[1]).transpose(1, 0, 2)
        return out

    wf = np.stack([by_head(a[p1 + "wk1"].T), by_head(a[p1 + "wq1"].T), by_head(a[p1 + "wv1"].T), by_head(a[p1 + "wo1"]),
                   by_head(a[p1 + "wq2"].T), by_head(a[p1 + "wk2"].T), by_head(a[p1 + "wv2"].T), by_head(a[p1 + "wo2"])], 1)

    negsel = np.zeros(128, f)
    negsel[32:64] = -1.0
    cols = {"eps": np.full(128, EPS, f), "negsel": negsel, "bo0": a["L0_xattn_bo"], "b1o1": a[p1 + "bo1"],
            "b1o2": a[p1 + "bo2"], "bf2": a[p1 + "b_ff2"], "b2q": b2[0:128], "b2k": b2[128:256],
            "b2so": a[p2 + "b_so"], "b2co": a[p2 + "b_co"], "b23": a[p2 + "b3"], "l2g": a[p2 + "ln_g"],
            "l2b": a[p2 + "ln_b"], "b3q": b3[0:128], "b3k": b3[128:256], "b3p": a[p3 + "proj_b"],
            "b3o": a[p3 + "out_b"], "b32": a[p3 + "mlp2_b"]}
    for i in "123":
        cols[f"l1g{i}"], cols[f"l1b{i}"] = a[p1 + f"ln{i}_g"], a[p1 + f"ln{i}_b"]
        cols[f"l3g{i}"], cols[f"l3b{i}"] = a[p3 + f"ln{i}_w"], a[p3 + f"ln{i}_b"]
    for t in range(8):
        cols[f"bf1_{t}"] = a[p1 + "b_ff1"][128 * t:128 * t + 128]
    for t in range(4):
        part = slice(128 * t, 128 * t + 128)
        cols[f"b21_{t}"], cols[f"b22_{t}"] = a[p2 + "b1"][part], a[p2 + "b2"][part]
        cols[f"b31_{t}"] = a[p3 + "mlp1_b"][part]
    for n, b in enumerate((zero, a[p2 + "b_q"], a[p3 + "q_b"])):
        for g, col in enumerate(query_bias(b, n == 2)):
            cols[f"qr{n}_{g}"] = col
    bias = np.stack([cols[n] for n in BIAS], 1)

    const = np.zeros((128, CONST["end"]), f)
    const[:, CONST["ident"]:CONST["ident"] + 128] = np.eye(128)
    const[:, CONST["mean"]:CONST["mean"] + 128] = 1.0 / 128
    for j in range(4):
        const[32 * j + 16, CONST["sums"] + j] = 1.0
        for part in range(3):
            const[32 * part + 8 * j:32 * part + 8 * j + 8, CONST["mask4"] + j] = 1.0
        const[98, CONST["mask4"] + j] = 1.0
    for h in range(H):
        const[8 * h:8 * h + 8, CONST["mask16"] + h] = S8
    for g in range(4):
        const[16 * g:16 * g + 16, CONST["left4"] + g] = 1.0
        const[16 * g:16 * g + 16, CONST["left16"]:CONST["left16"] + 16] = np.eye(16)
    const[0:S, CONST["causal"]:CONST["causal"] + S] = np.triu(np.full((S, S), NEG, f), 1)

    ctx = a["ctx_768"]
    ctxT = np.ones((B, C + 1, T), f)
    ctxT[:, 0:C] = ctx.transpose(0, 2, 1)
    ctxN = np.zeros((B, 128, NT, C), f)
    for c in range(NT):
        ctxN[:, 0:TC[c], c] = ctx[:, TO[c]:TO[c] + TC[c]]
    tmask = np.broadcast_to(a["mask_BxS_bf0"].view(np.uint8)[None], (S, B, S))
    cmask = np.broadcast_to(a["mask_BxS2_bf0"].view(np.uint8)[:, None, :], (B, 4, T))
    tmask, cmask = (np.ascontiguousarray(m).view(np.int32) for m in (tmask, cmask))
    arrays = {"xT": a["x"].reshape(N, D).T, "ctxT": ctxT, "ctxN": ctxN, "w0": w0, "w2": w2, "w3": w3, "wf": wf,
              "ff1": a[p1 + "w_ff1"], "ff2": tiles(a[p1 + "w_ff2"]), "bias": bias, "const": const,
              "tmask": tmask, "cmask": cmask}
    arrays = {k: np.ascontiguousarray(v) for k, v in arrays.items()}
    nc = bacc.Bacc("TRN2", target_bir_lowering=False, num_devices=1)
    args = [nc.dram_tensor("in_" + k, v.shape, mybir.dt.from_np(v.dtype), kind="ExternalInput").ap() for k, v in arrays.items()]
    args.append(nc.dram_tensor("outT", (D, N), F32, kind="ExternalOutput").ap())
    build(nc, *args)
    r = run(nc, [{"in_" + k: v for k, v in arrays.items()}], core_ids=[0])
    return r.results[0]["outT"].T.reshape(B, S, D)
```
